# Optimizing a Trainium2 kernel written in Bass

```python
import numpy as np
import jax
import jax.numpy as jnp

def _softmax(x, axis=-1):
    return jax.nn.softmax(x, axis=axis)

def _gelu(x):
    return jax.nn.gelu(x, approximate=True)

def _silu(x):
    return jax.nn.silu(x)

def _sigmoid(x):
    return jax.nn.sigmoid(x)

def _layernorm(x, axis=-1, eps=1e-05):
    m = jnp.mean(x, axis=axis, keepdims=True)
    v = jnp.var(x, axis=axis, keepdims=True)
    return (x - m) / jnp.sqrt(v + eps)

def _scatter_add(tgt, idx, src, axis=0):
    return tgt.at[idx].add(src)

def _segment_sum(src, seg, n):
    return jax.ops.segment_sum(src, seg, n)
kernel_name = 'mk_seq_postln_d1_jaxref_r8_5db406'

def setup_inputs(seed: int=0):
    np.random.seed(seed)
    _w = jnp.asarray

    def _L0_attn_setup():
        import jax, jax.numpy as jnp
        import numpy as np
        D_MODEL = 128
        N_HEADS = 16
        FEAT_DIM = 16
        V_DIM = 64
        EPS = 1e-12

        def taylor_exp(x):
            d = x.shape[-1]
            rd = jnp.sqrt(jnp.float32(d))
            rrd = jnp.sqrt(rd)
            r2 = jnp.sqrt(jnp.float32(2.0))
            x2 = (x[..., :, None] * x[..., None, :]).reshape(*x.shape[:-1], d * d) / r2
            ones = jnp.ones(x.shape[:-1] + (1,), dtype=x.dtype)
            return jnp.concatenate([ones, x / rrd, x2 / rd], axis=-1)
        key = jax.random.key(seed)
        k0, k1, k2, k3, k4 = jax.random.split(key, 5)
        b, l = (2, 256)
        scale = 1.0 / np.sqrt(D_MODEL)
        return {'hidden_states': jax.random.normal(k0, (b, l, D_MODEL), dtype=jnp.float32), 'Wq': jax.random.normal(k1, (D_MODEL, N_HEADS * FEAT_DIM), dtype=jnp.float32) * scale, 'Wk': jax.random.normal(k2, (D_MODEL, N_HEADS * FEAT_DIM), dtype=jnp.float32) * scale, 'Wv': jax.random.normal(k3, (D_MODEL, N_HEADS * V_DIM), dtype=jnp.float32) * scale, 'Wo': jax.random.normal(k4, (N_HEADS * V_DIM, D_MODEL), dtype=jnp.float32) * scale}
    _L0_attn_in = _L0_attn_setup()

    def _L0_ffn_setup():
        import jax, jax.numpy as jnp
        import numpy as np
        TAU = 1.0
        K_ROUTE = 3
        EPS = 1e-08

        def _route_combine_weights(x_addr, U, k, tau):
            z = x_addr @ U.T
            topv, topi = jax.lax.top_k(z, k)
            w = jax.nn.softmax(topv / (tau + EPS), axis=1)
            N, L = z.shape
            rows = jnp.arange(N)[:, None]
            return jnp.zeros((N, L), z.dtype).at[rows, topi].add(w)

        def _mixture(inp, C, W):
            L = W.shape[0]
            y = jnp.zeros((inp.shape[0], W.shape[1]), inp.dtype)
            for e in range(L):
                y = y + C[:, e:e + 1] * (inp @ W[e].T)
            return y
        key = jax.random.key(seed)
        ks = jax.random.split(key, 8)
        B, T, D_in, H, D_out, L, d_addr = (8, 1024, 128, 128, 128, 12, 64)

        def unit_rows(k, L_, d_):
            U = jax.random.normal(k, (L_, d_), dtype=jnp.float32)
            U = U - U.mean(axis=1, keepdims=True)
            return U / (jnp.linalg.norm(U, axis=1, keepdims=True) + EPS)

        def norm_tape(k, shape):
            W = jax.random.normal(k, shape, dtype=jnp.float32)
            n = jnp.sqrt(jnp.sum(W * W, axis=tuple(range(1, W.ndim)), keepdims=True)) + 1e-12
            return W / n
        x = jax.random.normal(ks[0], (B, T, D_in), dtype=jnp.float32)
        P_w = jax.random.normal(ks[1], (d_addr, D_in), dtype=jnp.float32) / np.sqrt(D_in)
        U1 = unit_rows(ks[2], L, d_addr)
        U2 = unit_rows(ks[3], L, d_addr)
        U3 = unit_rows(ks[4], L, d_addr)
        W1 = norm_tape(ks[5], (L, H, D_in))
        W2 = norm_tape(ks[6], (L, D_out, H))
        b2 = norm_tape(ks[7], (L, D_out))
        return {'x': x, 'P_w': P_w, 'U1': U1, 'U2': U2, 'U3': U3, 'W1': W1, 'W2': W2, 'b2': b2}
    _L0_ffn_in = _L0_ffn_setup()
    _d = {'L0_attn_hidden_states': _L0_attn_in['hidden_states'], 'L0_attn_Wq': _L0_attn_in['Wq'], 'L0_attn_Wk': _L0_attn_in['Wk'], 'L0_attn_Wv': _L0_attn_in['Wv'], 'L0_attn_Wo': _L0_attn_in['Wo'], 'L0_ffn_P_w': _L0_ffn_in['P_w'], 'L0_ffn_U1': _L0_ffn_in['U1'], 'L0_ffn_U2': _L0_ffn_in['U2'], 'L0_ffn_U3': _L0_ffn_in['U3'], 'L0_ffn_W1': _L0_ffn_in['W1'], 'L0_ffn_W2': _L0_ffn_in['W2'], 'L0_ffn_b2': _L0_ffn_in['b2']}
    _x0 = _d['L0_attn_hidden_states']
    _d['L0_attn_hidden_states'] = jax.random.normal(jax.random.fold_in(jax.random.key(seed), 1), (1, 2048, 128), dtype=_x0.dtype)
    del _x0
    return _d

def reference(L0_attn_hidden_states, L0_attn_Wq, L0_attn_Wk, L0_attn_Wv, L0_attn_Wo, L0_ffn_P_w, L0_ffn_U1, L0_ffn_U2, L0_ffn_U3, L0_ffn_W1, L0_ffn_W2, L0_ffn_b2):

    def _L0_attn_ref(hidden_states, Wq, Wk, Wv, Wo):
        import jax, jax.numpy as jnp
        import numpy as np
        D_MODEL = 128
        N_HEADS = 16
        FEAT_DIM = 16
        V_DIM = 64
        EPS = 1e-12

        def taylor_exp(x):
            d = x.shape[-1]
            rd = jnp.sqrt(jnp.float32(d))
            rrd = jnp.sqrt(rd)
            r2 = jnp.sqrt(jnp.float32(2.0))
            x2 = (x[..., :, None] * x[..., None, :]).reshape(*x.shape[:-1], d * d) / r2
            ones = jnp.ones(x.shape[:-1] + (1,), dtype=x.dtype)
            return jnp.concatenate([ones, x / rrd, x2 / rd], axis=-1)
        b, l, _ = hidden_states.shape
        q = (hidden_states @ Wq).reshape(b, l, N_HEADS, FEAT_DIM).transpose(0, 2, 1, 3)
        k = (hidden_states @ Wk).reshape(b, l, N_HEADS, FEAT_DIM).transpose(0, 2, 1, 3)
        v = (hidden_states @ Wv).reshape(b, l, N_HEADS, V_DIM).transpose(0, 2, 1, 3)
        qf = taylor_exp(q)
        kf = taylor_exp(k)
        A = jnp.einsum('bhnf,bhmf->bhnm', qf, kf)
        A = jnp.tril(A)
        y = jnp.einsum('bhnm,bhme->bhne', A, v)
        z = 1.0 / (jnp.einsum('bhlf,bhlf->bhl', qf, jnp.cumsum(kf, axis=2)) + EPS)
        y = y * z[..., None]
        out = y.transpose(0, 2, 1, 3).reshape(b, l, N_HEADS * V_DIM) @ Wo
        return out

    def _L0_ffn_ref(x, P_w, U1, U2, U3, W1, W2, b2):
        import jax, jax.numpy as jnp
        import numpy as np
        TAU = 1.0
        K_ROUTE = 3
        EPS = 1e-08

        def _route_combine_weights(x_addr, U, k, tau):
            z = x_addr @ U.T
            topv, topi = jax.lax.top_k(z, k)
            w = jax.nn.softmax(topv / (tau + EPS), axis=1)
            N, L = z.shape
            rows = jnp.arange(N)[:, None]
            return jnp.zeros((N, L), z.dtype).at[rows, topi].add(w)

        def _mixture(inp, C, W):
            L = W.shape[0]
            y = jnp.zeros((inp.shape[0], W.shape[1]), inp.dtype)
            for e in range(L):
                y = y + C[:, e:e + 1] * (inp @ W[e].T)
            return y
        B, T, D = x.shape
        xf = x.reshape(B * T, D)
        xa = xf @ P_w.T
        C1 = _route_combine_weights(xa, U1, K_ROUTE, TAU)
        C2 = _route_combine_weights(xa, U2, K_ROUTE, TAU)
        C3 = _route_combine_weights(xa, U3, K_ROUTE, TAU)
        h = jax.nn.gelu(_mixture(xf, C1, W1), approximate=False)
        y = _mixture(h, C2, W2) + C3 @ b2
        return y.reshape(B, T, -1)
    x = L0_attn_hidden_states
    x = _layernorm(x + _L0_attn_ref(x, L0_attn_Wq, L0_attn_Wk, L0_attn_Wv, L0_attn_Wo), axis=-1)
    x = _layernorm(x + _L0_ffn_ref(x, L0_ffn_P_w, L0_ffn_U1, L0_ffn_U2, L0_ffn_U3, L0_ffn_W1, L0_ffn_W2, L0_ffn_b2), axis=-1)
    return x

_drawn_inputs = setup_inputs


def setup_inputs(seed=0):
    import zlib

    import numpy as np

    out = dict(_drawn_inputs(seed))
    spreads = {}
    factors = {'L0_ffn_U1': 8.0, 'L0_ffn_U2': 8.0, 'L0_ffn_W1': 8.0, 'L0_ffn_W2': 8.0}
    for name, (base, spread) in spreads.items():
        noise = np.random.default_rng([zlib.crc32(name.encode()), seed]).standard_normal(out[name].shape)
        drawn = base * np.exp(spread * noise) if base else spread * noise
        out[name] = jnp.asarray(drawn.astype(out[name].dtype))
    for name, factor in factors.items():
        out[name] = (out[name] * factor).astype(out[name].dtype)
    return out
```

```python
from contextlib import ExitStack

import numpy as np
import concourse.bass as bass
from concourse import mybir

F32 = mybir.dt.float32
BF16 = mybir.dt.bfloat16
ALU = mybir.AluOpType
ACT = mybir.ActivationFunctionType
AX_X = mybir.AxisListType.X

T, D = 2048, 128
NH, DK, DV = 16, 16, 64
P = 128
NCH = T // P
BODY = 4
NIT = NCH // BODY
PAIR = 2 * P
GRP = 512
NA = DK + 1
NF = NA * (NA + 1) // 2
NX = NF - P
KFW = P + 32
DE = DV + 1
VW = 96
HPG = 4
NG = NH // HPG
HPB = 7
EPS_Z, EPS_LN = 1e-12, 1e-5
NPIECE = 6
Q_PARTS = (0, 1, 0, 2, 0, 1)
K_PARTS = (0, 0, 1, 0, 2, 1)
KS = NPIECE * DK
NE, NR, TOPK = 12, 3, 3
EU = 4
NU = NE // EU
ZW = NE + 5
SENT = 3.0e38


def shape_constants():
    form = np.zeros((DK, NF), np.float32)
    bias = np.zeros(NF, np.float32)
    for d in range(NF // NA):
        for i in range(NA):
            for j in {i, (i + d) % NA}:
                if j < DK:
                    form[j, d * NA + i] = 0.25
                else:
                    bias[d * NA + i] = 1.0
    stacked = np.zeros((KS, NF), np.float32)
    for part in range(3):
        r = Q_PARTS.index(part) * DK
        stacked[r:r + DK] = form
    c = np.zeros((P, 2 * P + P + 32 + 4), np.float32)
    c[:, 0:P] = np.eye(P)
    c[:, P:2 * P] = np.triu(np.ones((P, P)))
    c[0:KS, 2 * P:2 * P + P] = stacked[:, 0:P]
    c[0:KS, 3 * P:3 * P + NX] = stacked[:, P:NF]
    c[:, 3 * P + 32] = bias[0:P]
    for j in range(HPG):
        c[32 * j:32 * j + NX, 3 * P + 33] = bias[P:NF]
    c[:, 3 * P + 34] = 1.0
    c[:, 3 * P + 35] = EPS_LN
    sentinels = np.tile(-SENT / 2.0 ** np.arange(5, dtype=np.float32), (P, NR, 1)).astype(np.float32)
    return c, sentinels


def count(it, k, per, extra):
    return it * (BODY * per) + (k * per + extra)


def row(tile, it, k):
    if isinstance(it, int):
        return tile[:, it * BODY + k]
    return tile[:, bass.ds(it * BODY + k, 1)].squeeze(1)


def columns(tile, it, k):
    if isinstance(it, int):
        return tile[:, (it * BODY + k) * P:(it * BODY + k + 1) * P]
    return tile[:, bass.ds(it * (BODY * P) + k * P, P)]


def block_kernel(nc, x, xT, wqk, wkv, wo, p_w, uT, w1T, w2T, b2, consts, sents, out):
    parts_dram = nc.dram_tensor("qk_parts", [3, 2, NH * DK, T], BF16, kind="Internal").ap()
    with ExitStack() as ctx:
        def sb(name, shape, dt=F32):
            return ctx.enter_context(nc.sbuf_tensor(name, shape, dt))

        def sem(name):
            return ctx.enter_context(nc.semaphore(name))

        bank = [ctx.enter_context(nc.psum_tensor(f"bank{b}", [P, 512], F32)) for b in range(8)]
        state_bank, prep_bank, out_bank = bank[0:3], bank[3:6], bank[6:8]

        x_all = sb("x_all", [P, NCH, D])
        xT_all = sb("xT_all", [D, T])
        wqk_sb = sb("wqk_sb", [D, 2 * NH * DK])
        wkv_sb = sb("wkv_sb", [D, NH * DV + NH * DK])
        wo_sb = sb("wo_sb", [P, NH * DV // P, D])
        cst = sb("cst", [P, 3 * P + 36])
        ident, mask = cst[:, 0:P], cst[:, P:2 * P]
        main_bias, rest_bias = cst[:, 3 * P + 32:3 * P + 33], cst[:, 3 * P + 33:3 * P + 34]
        one_col, eps_col = cst[:, 3 * P + 34:3 * P + 35], cst[:, 3 * P + 35:3 * P + 36]
        form_bf = sb("form_bf", [P, P + 32], BF16)
        pw_sb = sb("pw_sb", [64, D])
        uT_sb = sb("uT_sb", [64, NR * NE])
        route_w = sb("route_w", [D, P])
        b2_sb = sb("b2_sb", [P, D])
        w1_sb = sb("w1_sb", [D, NE * D])
        w2_sb = sb("w2_sb", [D, NE * D])
        sent_sb = sb("sent_sb", [P, NR, 5])

        hi = sb("hi", [P, 4, GRP], BF16)
        mid = sb("mid", [P, 4, GRP], BF16)
        low = sb("low", [P, 4, GRP], BF16)
        rem = sb("rem", [P, 4, GRP])
        q_st = [sb(f"q_st{b}", [KS, NH, PAIR], BF16) for b in range(2)]
        k_st = [sb(f"k_st{b}", [KS, NH, PAIR], BF16) for b in range(2)]

        xc = sb("xc", [D, P])
        qf = sb("qf", [P, NH, P])
        qx = sb("qx", [P, NG, P])
        sq = sb("sq", [P, NH, P])
        at = sb("at", [P, NH, P])
        v1 = sb("v1", [P, NH, VW])
        k2 = sb("k2", [P, NH, 2 * NA])
        ksum = sb("ksum", [P, NH])
        kdiag = sb("kdiag", [P, NH, NA])
        kf = sb("kf", [P, NH, KFW])
        st = sb("st", [P, NH, VW])
        sx = sb("sx", [P, NG, HPG, DE])
        den = sb("den", [P, NH])
        rden = sb("rden", [P, NH])
        yn = sb("yn", [P, NH, DV])
        yT = sb("yT", [P, NH * DV // P, P])
        res = sb("res", [P, D])
        stats = sb("stats", [P, 6])
        mv = sb("mv", [P, 2])
        sd = sb("sd", [P, 1])
        rs = sb("rs", [P, 1])
        x1c = sb("x1c", [P, D])
        x1T = sb("x1T", [D, P])
        x1_all = sb("x1_all", [P, NCH, D])
        x1T_all = sb("x1T_all", [D, T])
        zc = sb("zc", [P, NR, ZW])
        top = sb("top", [P, NR, 8])
        zm = sb("zm", [P, NR, ZW])
        z_all = sb("z_all", [P, NCH, NR, NE])
        zm_all = sb("zm_all", [P, NCH, NR, NE])
        zmax_all = sb("zmax_all", [P, NCH, NR])

        io = [sem(f"loaded_{n}") for n in ("qk_in", "kv_in", "consts", "late", "ffn", "b2")]
        in_qk, in_kv, in_cst, in_late, in_ffn, in_b2 = io
        proj_done, hi_ready, rem_ready = sem("proj_done"), sem("hi_ready"), sem("rem_ready")
        mid_ready, low_ready = sem("mid_ready"), sem("low_ready")
        stored = [sem(f"parts_stored{t}") for t in range(4)]
        stacked = [sem(f"stacked{b}") for b in range(2)]
        init_v, init_g = sem("init_vector"), sem("init_gpsimd")
        qf_done, qx_done, s_done, kv_done = sem("qf_done"), sem("qx_done"), sem("s_done"), sem("kv_done")
        y_done, st_done, yt_done, wo_done = sem("y_done"), sem("st_done"), sem("yt_done"), sem("wo_done")
        x1t_done, z_done, rw_done = sem("x1t_done"), sem("z_done"), sem("rw_done")
        qf_ready, qx_ready, sq_ready, v_ready = sem("qf_ready"), sem("qx_ready"), sem("sq_ready"), sem("v_ready")
        st_ready, yt_ready, sd_ready, x1t_ready = sem("st_ready"), sem("yt_ready"), sem("sd_ready"), sem("x1t_ready")
        at_ready, k2_ready, kd_ready, kp_ready = sem("at_ready"), sem("k2_ready"), sem("kd_ready"), sem("kp_ready")
        yn_ready, res_ready, var_ready, x1_ready = sem("yn_ready"), sem("res_ready"), sem("var_ready"), sem("x1_ready")
        z_ready, xc_ready, rw_ready = sem("z_ready"), sem("xc_ready"), sem("rw_ready")
        x1_saved, zsaved = sem("x1_saved"), sem("z_saved")
        dve_step = sem("dve_step")
        passed = sem("passed")

        x1t_saved = sem("x1t_saved")
        N_INIT_V, N_INIT_G = 4, 6

        with nc.Block() as block:
            @block.sync
            def _(sp):
                sp.dma_start(wqk_sb[:], wqk).then_inc(in_qk, 16)
                sp.dma_start(xT_all[:], xT).then_inc(in_qk, 16)
                sp.dma_start(cst[:], consts).then_inc(in_cst, 16)
                sp.dma_start(wkv_sb[:], wkv).then_inc(in_kv, 16)
                sp.dma_start(x_all[:], x.rearrange("(c p) d -> p c d", p=P)).then_inc(in_late, 16)
                sp.dma_start(wo_sb[:], wo.rearrange("(t p) d -> p t d", p=P)).then_inc(in_late, 16)
                sp.dma_start(pw_sb[:], p_w).then_inc(in_late, 16)
                sp.dma_start(uT_sb[:], uT).then_inc(in_late, 16)
                sp.dma_start(sent_sb[:], sents).then_inc(in_late, 16)
                sp.dma_start(w1_sb[:], w1T).then_inc(in_ffn, 16)
                sp.dma_start(w2_sb[:], w2T).then_inc(in_ffn, 16)
                with sp.Fori(0, T // GRP) as g:
                    for t in range(4):
                        rows = slice((t % 2) * P, (t % 2) * P + P)
                        sp.wait_ge(hi_ready, g * 4 + (t + 1))
                        sp.wait_ge(mid_ready, g * 4 + (t + 1))
                        sp.wait_ge(low_ready, g * 4 + (t + 1))
                        for part, tile in enumerate((hi, mid, low)):
                            sp.dma_start(parts_dram[part, t // 2, rows, bass.ds(g * GRP, GRP)],
                                         tile[:, t, :]).then_inc(stored[t], 16)

                def load_pair(b, p):
                    for which, (dst, parts) in enumerate(((q_st[b], Q_PARTS), (k_st[b], K_PARTS))):
                        for j, part in enumerate(parts):
                            src = parts_dram[part, which, :, bass.ds(p * PAIR, PAIR)]
                            sp.dma_start(dst[j * DK:(j + 1) * DK, :, :],
                                         src.rearrange("(h i) n -> i h n", i=DK)).then_inc(stacked[b], 16)

                for t in range(4):
                    sp.wait_ge(stored[t], 48 * (T // GRP + 1))
                load_pair(0, 0)
                load_pair(1, 1)
                with sp.Fori(0, NIT - 1) as it:
                    for b in range(2):
                        sp.wait_ge(s_done, count(it, 2 * b + 2, NG, 0))
                        load_pair(b, it * 2 + (2 + b))

            @block.tensor
            def _(pe):
                pe.wait_ge(in_qk, 32)
                with pe.Fori(0, T // GRP) as g:
                    for t in range(4):
                        pe.wait_ge(rem_ready, g * 4 + (t + 1))
                        nc.tensor.matmul(bank[t][:], wqk_sb[:, t * P:(t + 1) * P], xT_all[:, bass.ds(g * GRP, GRP)],
                                         start=True, stop=True).then_inc(proj_done, 1)
                pe.wait_ge(in_late, 16 * 5)
                pe.wait_ge(init_v, N_INIT_V)
                nc.tensor.matmul(out_bank[0][:, 0:NR * NE], pw_sb[:], uT_sb[:], start=True, stop=True).then_inc(rw_done, 1)
                pe.wait_ge(init_g, N_INIT_G)
                pe.wait_ge(rem_ready, 4 * (T // GRP) + 4)
                st_flat, sx_flat = st[:].rearrange("p h e -> p (h e)"), sx[:].rearrange("p g j e -> p (g j e)")
                for b in range(3):
                    nc.tensor.matmul(state_bank[b][:], st_flat[:, 0:P], sx_flat[:, 0:512], start=True, stop=True)
                pe.wait_ge(rw_ready, 1)

                def query_features(it, k, g):
                    b, off = (k // 2) % 2, (k % 2) * P
                    nc.tensor.matmul(prep_bank[g % 3][:], form_bf[0:KS, 0:P],
                                     q_st[b][:, HPG * g:HPG * g + HPG, off:off + P],
                                     start=True, stop=True).then_inc(qf_done, 1)

                def query_rest(it, k):
                    b, off = (k // 2) % 2, (k % 2) * P
                    for j in range(HPG):
                        mm = nc.tensor.matmul(prep_bank[1][32 * j:32 * j + 32, :], form_bf[0:KS, P:P + 32],
                                              q_st[b][:, j:NH:HPG, off:off + P], start=True, stop=True)
                    mm.then_inc(qx_done, 1)

                def scores(it, k, g):
                    b, off = (k // 2) % 2, (k % 2) * P
                    for j in range(HPG):
                        h = HPG * g + j
                        mm = nc.tensor.matmul(prep_bank[(5 + g) % 3][:, j * P:(j + 1) * P],
                                              k_st[b][:, h, off:off + P], q_st[b][:, h, off:off + P],
                                              start=True, stop=True)
                    mm.then_inc(s_done, 1)

                def keys_values(it, k, u):
                    n = 512 if u < 2 else NH * DK
                    nc.tensor.matmul(prep_bank[u][:, 0:n], xc[:], wkv_sb[:, u * 512:u * 512 + n],
                                     start=True, stop=True).then_inc(kv_done, 1)

                def prep_group(it, k, g):
                    if g == 0:
                        pe.wait_ge(v_ready, count(it, k, 2, 1))
                        if k % 2 == 0:
                            pe.wait_ge(stacked[(k // 2) % 2], (it + (k // BODY + 1)) * (2 * NPIECE * 16))
                    if g == 1:
                        pe.wait_ge(v_ready, count(it, k, 2, 2))
                    if g == 2:
                        pe.wait_ge(k2_ready, count(it, k, 1, 1))
                    if g == 3:
                        pe.wait_ge(qf_ready, count(it, k, NG, 1))
                    query_features(it, k, g)

                def prep_rest(it, k):
                    pe.wait_ge(qf_ready, count(it, k, NG, 2))
                    query_rest(it, k)

                def prep_scores(it, k, g):
                    if g < 2:
                        pe.wait_ge(qf_ready, count(it, k, NG, 3 + g))
                    elif g == 2:
                        pe.wait_ge(qx_ready, count(it, k, 1, 1))
                    else:
                        pe.wait_ge(sq_ready, count(it, k, NG, 1))
                    scores(it, k, g)

                def prep_kv(it, k, u):
                    pe.wait_ge(sq_ready, count(it, k, NG, 2 + u))
                    if u == 0:
                        pe.wait_ge(in_kv, 16)
                        pe.wait_ge(xc_ready, count(it, k, 1, 1))
                    keys_values(it, k, u)

                def attend(it, k, g):
                    ob = out_bank[(9 * k + g) % 2]
                    if g == 0:
                        pe.wait_ge(x1t_ready, count(it, k, 1, 1))
                        pe.wait_ge(st_ready, count(it, k, 1, 1))
                        pe.wait_ge(qx_ready, count(it, k, 1, 1))
                        pe.wait_ge(v_ready, count(it, k, 2, 4))
                    elif g == 1:
                        pe.wait_ge(z_ready, count(it, k, 1, 1))
                    else:
                        pe.wait_ge(yn_ready, count(it, k, NG, g - 1))
                    pe.wait_ge(qf_ready, count(it, k, NG, g + 1))
                    pe.wait_ge(at_ready, count(it, k, NG, g + 1))
                    nc.tensor.matmul(ob[:, 0:HPG * DE], qx[:, g, :], sx[:, g, :, :].rearrange("p a b -> p (a b)"),
                                     start=True, stop=False, skip_group_check=True)
                    for j in range(HPG):
                        h = HPG * g + j
                        o = ob[:, j * DE:j * DE + VW]
                        nc.tensor.matmul(o, qf[:, h, :], st[:, h, :], start=False, stop=False, skip_group_check=True)
                        mm = nc.tensor.matmul(o, at[:, h, :], v1[:, h, :], start=False, stop=(j == HPG - 1),
                                              skip_group_check=True)
                    mm.then_inc(y_done, 1)

                def grow_state(it, k, heads):
                    if heads[0] == 0:
                        pe.wait_ge(kd_ready, count(it, k, 1, 1))
                        pe.wait_ge(kp_ready, count(it, k, 1, 2))
                    for h in heads:
                        o = state_bank[h // HPB][:, (h % HPB) * DE:(h % HPB) * DE + VW]
                        mm = nc.tensor.matmul(o, kf[:, h, 0:P], v1[:, h, :], start=False, stop=True,
                                              skip_group_check=True)
                        if h == HPB - 1:
                            mm.then_inc(st_done, 1)
                    if heads[-1] == NH - 1:
                        for h in range(NH):
                            g, j = h // HPG, h % HPG
                            o = state_bank[2][32 * j:32 * j + 32, (2 + g) * DE:(2 + g) * DE + VW]
                            mm = nc.tensor.matmul(o, kf[:, h, P:KFW], v1[:, h, :], start=False, stop=True,
                                                  skip_group_check=True)
                        mm.then_inc(st_done, 1)

                def turn_y(it, k, u):
                    ob = out_bank[(9 * k + 4 + u) % 2]
                    pe.wait_ge(yn_ready, count(it, k, NG, 4 if u else 3))
                    for j in range(4):
                        y2 = yn[:].rearrange("p h e -> p (h e)")
                        mm = nc.tensor.transpose(ob[:, j * P:(j + 1) * P], y2[:, (4 * u + j) * P:(4 * u + j + 1) * P], ident)
                    mm.then_inc(yt_done, 1)

                def project_y(it, k):
                    ob = out_bank[(9 * k + 6) % 2]
                    pe.wait_ge(yt_ready, count(it, k, 2, 2))
                    for j in range(8):
                        mm = nc.tensor.matmul(ob[:, 0:D], yT[:, j, :], wo_sb[:, j, :], start=(j == 0), stop=(j == 7))
                    mm.then_inc(wo_done, 1)

                def turn_x1(it, k):
                    ob = out_bank[(9 * k + 7) % 2]
                    pe.wait_ge(x1_ready, count(it, k, 1, 1))
                    nc.tensor.transpose(ob[:, 0:P], x1c[:], ident).then_inc(x1t_done, 1)

                def route(it, k):
                    ob = out_bank[(9 * k + 8) % 2]
                    pe.wait_ge(x1t_ready, count(it, k, 1, 2))
                    nc.tensor.matmul(ob[:, 0:P], x1T[:], route_w[:], start=True, stop=True).then_inc(z_done, 1)

                def chunk(it, k, last=False):
                    n = k + 1
                    for g in range(NG):
                        attend(it, k, g)
                        if not last:
                            prep_group(it, n, g)
                    grow_state(it, k, range(0, 8))
                    if not last:
                        prep_rest(it, n)
                        prep_scores(it, n, 0)
                        prep_scores(it, n, 1)
                    turn_y(it, k, 0)
                    turn_y(it, k, 1)
                    grow_state(it, k, range(8, NH))
                    if not last:
                        prep_scores(it, n, 2)
                        prep_scores(it, n, 3)
                    project_y(it, k)
                    if not last:
                        prep_kv(it, n, 0)
                        prep_kv(it, n, 1)
                    turn_x1(it, k)
                    if not last:
                        prep_kv(it, n, 2)
                    route(it, k)

                for g in range(NG):
                    prep_group(0, 0, g)
                prep_rest(0, 0)
                for g in range(NG):
                    prep_scores(0, 0, g)
                for u in range(3):
                    prep_kv(0, 0, u)
                with pe.Fori(0, NIT - 1) as it:
                    for k in range(BODY):
                        chunk(it, k)
                for k in range(BODY):
                    chunk(NIT - 1, k, last=(k == BODY - 1))

            @block.scalar
            def _(act):
                def part(t, dst, src, ready):
                    nc.scalar.activation(dst[:, t, :], src, ACT.Copy).then_inc(ready, 1)

                act.sem_inc(st_ready, 1)
                act.sem_inc(v_ready, 2)
                act.sem_inc(x1t_ready, 1)
                for t in range(4):
                    act.sem_inc(stored[t], 48)
                with act.Fori(0, T // GRP) as g:
                    def high(t):
                        act.wait_ge(proj_done, g * 4 + (t + 1))
                        act.wait_ge(stored[t], (g + 1) * 48)
                        part(t, hi, bank[t][:], hi_ready)

                    def middle(t):
                        act.wait_ge(rem_ready, g * 4 + (t + 5))
                        part(t, mid, rem[:, t, :], mid_ready)

                    high(0)
                    for t in range(1, 4):
                        high(t)
                        middle(t - 1)
                    middle(3)
                act.wait_ge(in_cst, 16)

                def query_squares(it, k, g):
                    act.wait_ge(qf_done, count(it, k, NG, g + 1))
                    nc.scalar.activation(qf[:, HPG * g:HPG * g + HPG, :], prep_bank[g % 3][:].rearrange("p (h n) -> p h n", h=HPG),
                                         ACT.Square, bias=main_bias).then_inc(qf_ready, 1)

                def rest_squares(it, k):
                    act.wait_ge(qx_done, count(it, k, 1, 1))
                    nc.scalar.activation(qx[:], prep_bank[1][:].rearrange("p (g n) -> p g n", g=NG),
                                         ACT.Square, bias=rest_bias).then_inc(qx_ready, 1)

                def score_squares(it, k, g, first=False):
                    act.wait_ge(s_done, count(it, k, NG, g + 1))
                    if not first:
                        act.wait_ge(at_ready, count(it, k, NG, g - 3))
                    nc.scalar.activation(sq[:, HPG * g:HPG * g + HPG, :], prep_bank[(5 + g) % 3][:].rearrange("p (h n) -> p h n", h=HPG),
                                         ACT.Square, bias=one_col, scale=0.25).then_inc(sq_ready, 1)

                def take_values(it, k, u):
                    act.wait_ge(kv_done, count(it, k, 3, u + 1))
                    nc.scalar.activation(v1[:, 8 * u:8 * u + 8, 0:DV], prep_bank[u][:].rearrange("p (h e) -> p h e", e=DV),
                                         ACT.Copy).then_inc(v_ready, 1)

                def take_state(it, k, half):
                    act.wait_ge(st_done, count(it, k, 2, half + 1))
                    for b in ((0,), (1, 2))[half]:
                        n = min(HPB, NH - HPB * b)
                        nc.scalar.activation(st[:, HPB * b:HPB * b + n, 0:DE],
                                             state_bank[b][:, 0:n * DE].rearrange("p (h e) -> p h e", e=DE), ACT.Copy)
                    if half:
                        for j in range(HPG):
                            rows = slice(32 * j, 32 * j + 32)
                            last = nc.scalar.activation(sx[rows, :, j, :],
                                                        state_bank[2][rows, 2 * DE:(2 + NG) * DE].rearrange("p (g e) -> p g e", e=DE),
                                                        ACT.Copy)
                        last.then_inc(st_ready, 1)

                def take_turned_y(it, k, u):
                    act.wait_ge(yt_done, count(it, k, 2, u + 1))
                    nc.scalar.activation(yT[:, 4 * u:4 * u + 4, :],
                                         out_bank[(9 * k + 4 + u) % 2][:].rearrange("p (j n) -> p j n", j=4),
                                         ACT.Copy).then_inc(yt_ready, 1)

                def deviation(it, k):
                    act.wait_ge(var_ready, count(it, k, 1, 1))
                    nc.scalar.activation(sd[:], mv[:, 1:2], ACT.Sqrt, bias=eps_col).then_inc(sd_ready, 1)

                def take_turned_x1(it, k):
                    act.wait_ge(x1t_done, count(it, k, 1, 1))
                    act.wait_ge(x1t_saved, count(it, k, 1, 1))
                    nc.scalar.activation(x1T[:], out_bank[(9 * k + 7) % 2][:, 0:P], ACT.Copy).then_inc(x1t_ready, 1)

                def chunk(it, k, last=False):
                    n = k + 1
                    if not last:
                        for g in range(NG):
                            query_squares(it, n, g)
                    if not last:
                        take_state(it, k, 0)
                        rest_squares(it, n)
                        score_squares(it, n, 0)
                        score_squares(it, n, 1)
                    take_turned_y(it, k, 0)
                    take_turned_y(it, k, 1)
                    if not last:
                        score_squares(it, n, 2)
                        score_squares(it, n, 3)
                        take_state(it, k, 1)
                    deviation(it, k)
                    if not last:
                        take_values(it, n, 0)
                        take_values(it, n, 1)
                    take_turned_x1(it, k)

                for g in range(NG):
                    query_squares(0, 0, g)
                rest_squares(0, 0)
                for g in range(NG):
                    score_squares(0, 0, g, first=True)
                take_values(0, 0, 0)
                take_values(0, 0, 1)
                with act.Fori(0, NIT - 1) as it:
                    for k in range(BODY):
                        chunk(it, k)
                for k in range(BODY):
                    chunk(NIT - 1, k, last=(k == BODY - 1))

            @block.vector
            def _(dve):
                dve.sem_inc(rem_ready, 4)
                dve.sem_inc(k2_ready, 1)
                dve.sem_inc(z_ready, 1)
                dve.wait_ge(in_cst, 16)
                nc.vector.tensor_copy(form_bf[:], cst[:, 2 * P:3 * P + 32]).then_inc(init_v, 1)
                nc.vector.memset(route_w[:], 0.0).then_inc(init_v, 1)
                nc.vector.memset(k2[:, :, DK:2 * NA:NA], 1.0).then_inc(init_v, 1)
                with dve.Fori(0, T // GRP) as g:
                    def remainder(t):
                        dve.wait_ge(hi_ready, g * 4 + (t + 1))
                        nc.vector.tensor_tensor(rem[:, t, :], bank[t][:], hi[:, t, :], ALU.subtract).then_inc(rem_ready, 1)

                    def lowest(t):
                        dve.wait_ge(mid_ready, g * 4 + (t + 1))
                        nc.vector.tensor_tensor(low[:, t, :], rem[:, t, :], mid[:, t, :], ALU.subtract).then_inc(low_ready, 1)

                    remainder(0)
                    for t in range(1, 4):
                        remainder(t)
                        lowest(t - 1)
                    lowest(3)
                dve.wait_ge(in_late, 16 * 5)
                nc.vector.tensor_copy(zc[:, :, NE:ZW], sent_sb[:]).then_inc(init_v, 1)
                dve.wait_ge(rw_done, 1)
                dve.wait_ge(init_v, N_INIT_V)
                nc.vector.tensor_copy(route_w[:, 0:NR * NE], out_bank[0][:, 0:NR * NE]).then_inc(rw_ready, 1)

                BEFORE, PER = 3, 17
                at_chunk = [0, 0, -BEFORE]

                def step(ins):
                    it, k, done = at_chunk
                    ins.then_inc(dve_step, 1)
                    at_chunk[2] = done + 1
                    dve.wait_ge(dve_step, count(it, k, PER, BEFORE + done + 1))

                def normalize(it, k, g):
                    ob = out_bank[(9 * k + g) % 2][:, 0:HPG * DE].rearrange("p (h e) -> p h e", e=DE)
                    heads = slice(HPG * g, HPG * g + HPG)
                    dve.wait_ge(y_done, count(it, k, NG, g + 1))
                    step(nc.vector.tensor_scalar(den[:, heads], ob[:, :, DV], 2 * EPS_Z, None, ALU.add))
                    step(nc.vector.reciprocal(rden[:, heads], den[:, heads]))
                    nc.vector.tensor_tensor(yn[:, heads, :], ob[:, :, 0:DV],
                                            rden[:, heads].unsqueeze(2).broadcast_to([P, HPG, DV]),
                                            ALU.mult).then_inc(yn_ready, 1)

                def mask_scores(it, k, g):
                    heads = slice(HPG * g, HPG * g + HPG)
                    dve.wait_ge(sq_ready, count(it, k, NG, g + 1))
                    nc.vector.scalar_tensor_tensor(out=at[:, heads, :], in0=sq[:, heads, :], scalar=1.0,
                                                   in1=mask.unsqueeze(1).broadcast_to([P, HPG, P]),
                                                   op0=ALU.add, op1=ALU.mult).then_inc(at_ready, 1)

                def take_keys(it, k):
                    kb = prep_bank[2][:, 0:NH * DK].rearrange("p (h i) -> p h i", i=DK)
                    dve.wait_ge(kv_done, count(it, k, 3, 3))
                    dve.wait_ge(kp_ready, count(it, k, 1, 1))
                    nc.vector.tensor_copy(k2[:, :, 0:DK], kb)
                    nc.vector.tensor_copy(k2[:, :, NA:NA + DK], kb).then_inc(k2_ready, 1)

                def key_diagonal(it, k):
                    dve.wait_ge(k2_ready, count(it, k, 1, 2))
                    step(nc.vector.reduce_sum(ksum[:], k2[:, :, 0:NA], AX_X))
                    step(nc.vector.scalar_tensor_tensor(out=kdiag[:], in0=k2[:, :, 0:NA], scalar=2.0,
                                                               in1=ksum[:].unsqueeze(2).broadcast_to([P, NH, NA]),
                                                               op0=ALU.mult, op1=ALU.subtract))
                    step(nc.vector.tensor_tensor(kf[:, :, 0:NA], kdiag[:], k2[:, :, 0:NA], ALU.mult))
                    nc.vector.tensor_scalar(kf[:, :, DK], kf[:, :, DK], 1.0, None, ALU.add).then_inc(kd_ready, 1)

                def add_residual(it, k):
                    dve.wait_ge(wo_done, count(it, k, 1, 1))
                    step(nc.vector.tensor_tensor(res[:], out_bank[(9 * k + 6) % 2][:, 0:D],
                                                        row(x_all, it, k), ALU.add))
                    step(nc.vector.bn_stats(stats[:], res[:]))
                    dve.sem_inc(passed, 1)
                    nc.vector.bn_aggr(mv[:], stats[:]).then_inc(var_ready, 1)

                def norm(it, k):
                    dve.wait_ge(sd_ready, count(it, k, 1, 1))
                    step(nc.vector.reciprocal(rs[:], sd[:]))
                    dve.wait_ge(x1_saved, count(it, k, 1, 1))
                    nc.vector.tensor_scalar(x1c[:], res[:], mv[:, 0:1], rs[:], ALU.subtract, ALU.mult).then_inc(x1_ready, 1)

                def take_routes(it, k):
                    dve.wait_ge(z_done, count(it, k, 1, 1))
                    nc.vector.tensor_copy(zc[:, :, 0:NE], out_bank[(9 * k + 8) % 2][:, 0:NR * NE].rearrange("p (r e) -> p r e", e=NE))\
                      .then_inc(z_ready, 1)

                def choose(it, k):
                    dve.wait_ge(z_ready, count(it, k, 1, 2))
                    dve.sem_inc(passed, 1)
                    for r in range(NR):
                        mx = nc.vector.max(out=top[:, r, :], in_=zc[:, r, 0:NE])
                    step(mx)
                    nc.vector.tensor_copy(row(zmax_all, it, k), top[:, :, 0])
                    step(nc.vector.tensor_copy(top[:, :, TOPK:8], sent_sb[:]))
                    dve.sem_inc(passed, 1)
                    for r in range(NR):
                        mr = nc.vector.match_replace(out=zm[:, r, :], in_to_replace=top[:, r, :], in_values=zc[:, r, :], imm_value=SENT)
                    step(mr)
                    nc.vector.tensor_copy(row(z_all, it, k), zc[:, :, 0:NE])
                    nc.vector.tensor_copy(row(zm_all, it, k), zm[:, :, 0:NE]).then_inc(zsaved, 1)

                def chunk(it, k, last=False):
                    n = k + 1
                    at_chunk[:] = [it, k, 0]
                    for g in range(NG):
                        normalize(it, k, g)
                    if not last:
                        for g in range(NG):
                            mask_scores(it, n, g)
                    add_residual(it, k)
                    norm(it, k)
                    if not last:
                        take_keys(it, n)
                    take_routes(it, k)
                    choose(it, k)
                    if not last:
                        key_diagonal(it, n)
                        assert at_chunk[2] == PER

                for g in range(NG):
                    mask_scores(0, 0, g)
                take_keys(0, 0)
                key_diagonal(0, 0)
                with dve.Fori(0, NIT - 1) as it:
                    for k in range(BODY):
                        chunk(it, k)
                for k in range(BODY):
                    chunk(NIT - 1, k, last=(k == BODY - 1))

            @block.gpsimd
            def _(pool):
                nc.gpsimd.memset(st[:], 0.0).then_inc(init_g, 1)
                nc.gpsimd.memset(sx[:], 0.0).then_inc(init_g, 1)
                nc.gpsimd.memset(v1[:], 0.0).then_inc(init_g, 1)
                nc.gpsimd.memset(kf[:], 0.0).then_inc(init_g, 1)
                nc.gpsimd.memset(b2_sb[:], 0.0).then_inc(init_g, 1)
                pool.wait_ge(init_g, N_INIT_G - 1)
                nc.gpsimd.memset(v1[:, :, DV], 1.0).then_inc(init_g, 1)
                pool.sem_inc(kp_ready, 1)
                pool.sem_inc(x1_saved, 1)
                pool.sem_inc(x1t_saved, 1)
                pool.wait_ge(init_g, N_INIT_G)
                pool.dma_start(b2_sb[0:NE, :], b2).then_inc(in_b2, 16)

                def take_x(it, k, first=False):
                    if not first:
                        pool.wait_ge(kv_done, count(it, k, 3, 0))
                    nc.gpsimd.tensor_copy(xc[:], columns(xT_all, it, k)).then_inc(xc_ready, 1)

                def key_products(it, k):
                    pool.wait_ge(k2_ready, count(it, k, 1, 2))
                    whole = k2[:]
                    ahead = bass.AP(whole.tensor, whole.offset + 1,
                                    [whole.ap[0], (2 * NA, NH), (1, NF // NA - 1), (1, NA)])
                    here = k2[:, :, 0:NA].unsqueeze(2).broadcast_to([P, NH, NF // NA - 1, NA])
                    out4 = kf[:, :, NA:NF].rearrange("p h (d i) -> p h d i", i=NA)
                    nc.gpsimd.tensor_tensor(out4, here, ahead, ALU.mult).then_inc(kp_ready, 1)

                def keep_x1(it, k):
                    pool.wait_ge(x1_ready, count(it, k, 1, 1))
                    nc.gpsimd.tensor_copy(row(x1_all, it, k), x1c[:]).then_inc(x1_saved, 1)
                    pool.wait_ge(x1t_ready, count(it, k, 1, 2))
                    nc.gpsimd.tensor_copy(columns(x1T_all, it, k), x1T[:]).then_inc(x1t_saved, 1)

                pool.wait_ge(in_qk, 32)
                take_x(0, 0, first=True)
                pool.wait_ge(init_v, 3)
                key_products(0, 0)
                with pool.Fori(0, NIT - 1) as it:
                    for k in range(BODY):
                        take_x(it, k + 1)
                        keep_x1(it, k)
                        key_products(it, k + 1)
                for k in range(BODY):
                    if k < BODY - 1:
                        take_x(NIT - 1, k + 1)
                    keep_x1(NIT - 1, k)
                    if k < BODY - 1:
                        key_products(NIT - 1, k + 1)

        ex = sb("ex", [P, NCH * NR, NE])
        wsum = sb("wsum", [P, NCH * NR])
        wr = sb("wr", [P, NCH * NR])
        mix_all = sb("mix_all", [P, NCH, NR, NE])
        xb = [sb(f"xb{b}", [D, P]) for b in range(BODY)]
        cw = [sb(f"cw{b}", [P, NR, NE]) for b in range(BODY)]
        c3 = [sb(f"c3{b}", [P, P]) for b in range(BODY)]
        acc = sb("acc", [P, 4, D])
        hsum = [sb(f"hsum{b}", [P, D]) for b in range(2)]
        hh = [sb(f"hh{b}", [P, D]) for b in range(2)]
        hT = sb("hT", [P, P])
        c3T = sb("c3T", [P, P])
        ysum = sb("ysum", [P, 2, D])
        ostats, omv, osd, ors = sb("ostats", [P, 6]), sb("omv", [P, 2]), sb("osd", [P, 1]), sb("ors", [P, 1])
        oc = [sb(f"oc{b}", [P, D]) for b in range(BODY)]

        c3_init, mix_step, sh_ready, ex_ready, mix_ready = (sem(n) for n in ("c3_init", "mix_step", "sh_ready", "ex_ready", "mix_ready"))
        xb_ready, l1_done, l2_done, turned, took = (sem(n) for n in ("xb_ready", "l1_done", "l2_done", "turned", "took"))
        b2_done, comb1, comb2, hsum_ready, h_ready = (sem(n) for n in ("b2_done", "comb1", "comb2", "hsum_ready", "h_ready"))
        b2_read, ovar_ready, osd_ready, oc_ready, ostep = (sem(n) for n in ("b2_read", "ovar_ready", "osd_ready", "oc_ready", "ostep"))
        out_saved = [sem(f"out_saved{b}") for b in range(BODY)]

        with nc.Block() as block:
            @block.sync
            def _(sp):
                for k in range(BODY):
                    sp.sem_inc(out_saved[k], 16)
                with sp.Fori(0, NIT) as it:
                    for k in range(BODY):
                        sp.wait_ge(oc_ready, count(it, k, 1, 1))
                        sp.dma_start(out[bass.ds(it * (BODY * P) + k * P, P), :], oc[k][:]).then_inc(out_saved[k], 16)
                for k in range(BODY):
                    sp.wait_ge(out_saved[k], 16 * (NIT + 1))

            @block.gpsimd
            def _(pool):
                for b in range(BODY):
                    nc.gpsimd.memset(c3[b][:], 0.0).then_inc(c3_init, 1)
                pool.wait_ge(c3_init, BODY)

                def stage(it, k, first=False):
                    if not first:
                        pool.wait_ge(comb2, count(it, k, NE, -2 * NE))
                    nc.gpsimd.tensor_copy(xb[k % BODY][:], columns(x1T_all, it, k)).then_inc(xb_ready, 1)
                    if first and k == 0:
                        pool.wait_ge(mix_ready, 1)
                    nc.gpsimd.tensor_copy(cw[k % BODY][:], row(mix_all, it, k)).then_inc(xb_ready, 1)
                    nc.gpsimd.tensor_copy(c3[k % BODY][:, 0:NE], row(mix_all, it, k)[:, 2, :]).then_inc(xb_ready, 1)

                for k in range(BODY):
                    stage(0, k, first=True)
                with pool.Fori(0, NIT - 1) as it:
                    for k in range(BODY):
                        stage(it, k + BODY)

            @block.tensor
            def _(pe):
                def first(it, k):
                    pe.wait_ge(xb_ready, count(it, k, 3, 1))
                    for u in range(NU):
                        pe.wait_ge(comb1, count(it, k, NE, EU * (u + 1)))
                        nc.tensor.matmul(bank[u][:], xb[k % BODY][:], w1_sb[:, u * 512:(u + 1) * 512],
                                         start=True, stop=True).then_inc(l1_done, 1)

                def turn(it, k):
                    pe.wait_ge(took, count(it, k, 2, 2))
                    pe.wait_ge(h_ready, count(it, k, 1, 1))
                    pe.wait_ge(xb_ready, count(it, k, 3, 3))
                    nc.tensor.transpose(bank[6][:, 0:P], hh[k % 2][:], ident)
                    nc.tensor.transpose(bank[6][:, P:2 * P], c3[k % BODY][:], ident).then_inc(turned, 1)

                def second(it, k):
                    pe.wait_ge(took, count(it, k, 2, 4))
                    for u in range(NU):
                        pe.wait_ge(comb2, count(it, k, NE, EU * (u + 1)))
                        nc.tensor.matmul(bank[3 + u][:], hT[:], w2_sb[:, u * 512:(u + 1) * 512],
                                         start=True, stop=True).then_inc(l2_done, 1)
                    pe.wait_ge(b2_read, count(it, k, 1, 1))
                    nc.tensor.matmul(bank[7][:, 0:D], c3T[:], b2_sb[:], start=True, stop=True).then_inc(b2_done, 1)

                pe.wait_ge(in_ffn, 32)
                pe.wait_ge(in_b2, 16)
                for k in range(3):
                    first(0, k)
                with pe.Fori(0, NIT - 1) as it:
                    for k in range(BODY):
                        turn(it, k)
                        second(it, k)
                        first(it, k + 3)
                for k in range(BODY):
                    turn(NIT - 1, k)
                    second(NIT - 1, k)
                    if k + 3 < BODY:
                        first(NIT - 1, k + 3)

            @block.scalar
            def _(act):
                act.sem_inc(took, 2)
                act.wait_ge(sh_ready, 1)
                nc.scalar.activation(ex[:], ex[:], ACT.Exp).then_inc(ex_ready, 1)

                def gelu(it, k):
                    act.wait_ge(hsum_ready, count(it, k, 1, 1))
                    nc.scalar.activation(hh[k % 2][:], hsum[k % 2][:], ACT.Gelu).then_inc(h_ready, 1)

                def take(it, k):
                    act.wait_ge(turned, count(it, k, 1, 1))
                    nc.scalar.activation(hT[:], bank[6][:, 0:P], ACT.Copy).then_inc(took, 1)
                    nc.scalar.activation(c3T[:], bank[6][:, P:2 * P], ACT.Copy).then_inc(took, 1)

                def deviation(it, k):
                    act.wait_ge(ovar_ready, count(it, k, 1, 1))
                    nc.scalar.activation(osd[:], omv[:, 1:2], ACT.Sqrt, bias=eps_col).then_inc(osd_ready, 1)

                gelu(0, 0)
                gelu(0, 1)
                with act.Fori(0, NIT - 1) as it:
                    for k in range(BODY):
                        take(it, k)
                        deviation(it, k)
                        gelu(it, k + 2)
                for k in range(BODY):
                    take(NIT - 1, k)
                    deviation(NIT - 1, k)
                    if k + 2 < BODY:
                        gelu(NIT - 1, k + 2)

            @block.vector
            def _(dve):
                dve.sem_inc(comb1, NE)
                dve.sem_inc(comb2, NE)
                dve.sem_inc(b2_read, 1)
                done = [0]

                def link(ins):
                    done[0] += 1
                    ins.then_inc(mix_step, 1)
                    dve.wait_ge(mix_step, done[0])

                z3 = z_all[:].rearrange("p c r e -> p (c r) e")
                zm3 = zm_all[:].rearrange("p c r e -> p (c r) e")
                mix3 = mix_all[:].rearrange("p c r e -> p (c r) e")
                zmax3 = zmax_all[:].rearrange("p c r -> p (c r)")
                wide = [P, NCH * NR, NE]
                nc.vector.tensor_tensor(ex[:], z3, zmax3.unsqueeze(2).broadcast_to(wide), ALU.subtract).then_inc(sh_ready, 1)
                dve.wait_ge(ex_ready, 1)
                link(nc.vector.scalar_tensor_tensor(out=mix3, in0=zm3, scalar=SENT, in1=ex[:], op0=ALU.is_equal, op1=ALU.mult))
                link(nc.vector.reduce_sum(wsum[:], mix3, AX_X))
                link(nc.vector.reciprocal(wr[:], wsum[:]))
                nc.vector.tensor_tensor(mix3, mix3, wr[:].unsqueeze(2).broadcast_to(wide), ALU.mult).then_inc(mix_ready, 1)

                def mixture(it, k, r, banks, done_sem, comb, seed=None):
                    dve.wait_ge(xb_ready, count(it, k, 3, 2))
                    for e in range(NE):
                        if e % EU == 0:
                            dve.wait_ge(done_sem, count(it, k, NU, e // EU + 1))
                        src = banks[e // EU][:, (e % EU) * D:(e % EU + 1) * D]
                        a, w = acc[:, 2 * r + e % 2, :], cw[k % BODY][:, r, e:e + 1]
                        if e >= 2:
                            dve.wait_ge(comb, count(it, k, NE, NE + e - 1))
                            ins = nc.vector.scalar_tensor_tensor(out=a, in0=src, scalar=w, in1=a, op0=ALU.mult, op1=ALU.add)
                        elif e == 0 and seed is not None:
                            ins = nc.vector.scalar_tensor_tensor(out=a, in0=src, scalar=w, in1=seed, op0=ALU.mult, op1=ALU.add)
                        else:
                            ins = nc.vector.tensor_scalar(a, src, w, None, ALU.mult)
                        ins.then_inc(comb, 1)

                def hidden(it, k, first=False):
                    if not first or k:
                        dve.wait_ge(hsum_ready, count(it, k, 1, 0))
                    mixture(it, k, 0, bank[0:3], l1_done, comb1)
                    if not first:
                        dve.wait_ge(h_ready, count(it, k, 1, -1))
                    dve.wait_ge(comb1, count(it, k, NE, 2 * NE))
                    nc.vector.tensor_tensor(hsum[k % 2][:], acc[:, 0, :], acc[:, 1, :], ALU.add).then_inc(hsum_ready, 1)

                OPER = 3
                at_chunk = [0, 0, 0]

                def step(ins):
                    it, k, n = at_chunk
                    ins.then_inc(ostep, 1)
                    at_chunk[2] = n + 1
                    dve.wait_ge(ostep, count(it, k, OPER, n + 1))

                def output_sum(it, k):
                    mixture(it, k, 1, bank[3:6], l2_done, comb2, seed=row(x1_all, it, k))
                    dve.wait_ge(comb2, count(it, k, NE, 2 * NE))
                    step(nc.vector.tensor_tensor(ysum[:, 0, :], acc[:, 2, :], acc[:, 3, :], ALU.add))
                    dve.wait_ge(b2_done, count(it, k, 1, 1))
                    nc.vector.tensor_tensor(ysum[:, 1, :], bank[7][:, 0:D], ysum[:, 0, :], ALU.add).then_inc(b2_read, 1)
                    dve.wait_ge(b2_read, count(it, k, 1, 2))
                    step(nc.vector.bn_stats(ostats[:], ysum[:, 1, :]))
                    dve.sem_inc(passed, 1)
                    nc.vector.bn_aggr(omv[:], ostats[:]).then_inc(ovar_ready, 1)

                def output(it, k):
                    dve.wait_ge(osd_ready, count(it, k, 1, 1))
                    step(nc.vector.reciprocal(ors[:], osd[:]))
                    dve.wait_ge(out_saved[k], (it + 1) * 16)
                    nc.vector.tensor_scalar(oc[k][:], ysum[:, 1, :], omv[:, 0:1], ors[:], ALU.subtract, ALU.mult).then_inc(oc_ready, 1)

                def chunk(it, k, last=False):
                    at_chunk[:] = [it, k, 0]
                    output_sum(it, k)
                    if not (last and k + 2 >= BODY):
                        hidden(it, k + 2)
                    output(it, k)
                    assert at_chunk[2] == OPER

                hidden(0, 0, first=True)
                hidden(0, 1, first=True)
                with dve.Fori(0, NIT - 1) as it:
                    for k in range(BODY):
                        chunk(it, k)
                for k in range(BODY):
                    chunk(NIT - 1, k, last=True)


def kernel(**inputs):
    import concourse.bacc as bacc
    from concourse.bass_utils import run_bass_kernel_spmd

    a = {n.removeprefix("L0_"): np.asarray(v) for n, v in inputs.items()}
    x = np.ascontiguousarray(a["attn_hidden_states"].reshape(T, D))
    consts, sents = shape_constants()
    arrays = {
        "x": x,
        "xT": np.ascontiguousarray(x.T),
        "wqk": np.concatenate([a["attn_Wq"], a["attn_Wk"]], axis=1),
        "wkv": np.concatenate([a["attn_Wv"], a["attn_Wk"]], axis=1),
        "wo": np.ascontiguousarray(a["attn_Wo"]),
        "p_w": np.ascontiguousarray(a["ffn_P_w"]),
        "uT": np.ascontiguousarray(np.concatenate([a["ffn_U1"], a["ffn_U2"], a["ffn_U3"]], axis=0).T),
        "w1T": np.ascontiguousarray(a["ffn_W1"].transpose(2, 0, 1).reshape(D, NE * D)),
        "w2T": np.ascontiguousarray(a["ffn_W2"].transpose(2, 0, 1).reshape(D, NE * D)),
        "b2": np.ascontiguousarray(a["ffn_b2"]),
        "consts": consts,
        "sents": sents,
    }
    nc = bacc.Bacc("TRN2", target_bir_lowering=False, num_devices=1)
    handles = [nc.dram_tensor(n, list(v.shape), F32, kind="ExternalInput").ap() for n, v in arrays.items()]
    out = nc.dram_tensor("out", [T, D], F32, kind="ExternalOutput").ap()
    block_kernel(nc, *handles, out)
    r = run_bass_kernel_spmd(nc, [arrays], core_ids=[0])
    return r.results[0]["out"].reshape(1, T, D)
```

```python
from contextlib import ExitStack

import numpy as np
import concourse.bass as bass
from concourse import mybir

F32 = mybir.dt.float32
BF16 = mybir.dt.bfloat16
ALU = mybir.AluOpType
ACT = mybir.ActivationFunctionType
AX_X = mybir.AxisListType.X

T, D = 2048, 128
NH, DK, DV = 16, 16, 64
P = 128
NCH = T // P
BODY = 4
NIT = NCH // BODY
PAIR = 2 * P
GRP = 512
NA = DK + 1
NF = NA * (NA + 1) // 2
NX = NF - P
KFW = P + 32
DE = DV + 1
VW = 96
HPG = 4
NG = NH // HPG
HPB = 7
EPS_Z, EPS_LN = 1e-12, 1e-5
NPIECE = 6
Q_PARTS = (0, 1, 0, 2, 0, 1)
K_PARTS = (0, 0, 1, 0, 2, 1)
KS = NPIECE * DK
NE, NR, TOPK = 12, 3, 3
EU = 4
NU = NE // EU
ZW = NE + 5
SENT = 3.0e38


def shape_constants():
    form = np.zeros((DK, NF), np.float32)
    bias = np.zeros(NF, np.float32)
    for d in range(NF // NA):
        for i in range(NA):
            for j in {i, (i + d) % NA}:
                if j < DK:
                    form[j, d * NA + i] = 0.25
                else:
                    bias[d * NA + i] = 1.0
    stacked = np.zeros((KS, NF), np.float32)
    for part in range(3):
        r = Q_PARTS.index(part) * DK
        stacked[r:r + DK] = form
    c = np.zeros((P, 2 * P + P + 32 + 4), np.float32)
    c[:, 0:P] = np.eye(P)
    c[:, P:2 * P] = np.triu(np.ones((P, P)))
    c[0:KS, 2 * P:2 * P + P] = stacked[:, 0:P]
    c[0:KS, 3 * P:3 * P + NX] = stacked[:, P:NF]
    c[:, 3 * P + 32] = bias[0:P]
    for j in range(HPG):
        c[32 * j:32 * j + NX, 3 * P + 33] = bias[P:NF]
    c[:, 3 * P + 34] = 1.0
    c[:, 3 * P + 35] = EPS_LN
    sentinels = np.tile(-SENT / 2.0 ** np.arange(5, dtype=np.float32), (P, NR, 1)).astype(np.float32)
    return c, sentinels


def count(it, k, per, extra):
    return it * (BODY * per) + (k * per + extra)


def row(tile, it, k):
    if isinstance(it, int):
        return tile[:, it * BODY + k]
    return tile[:, bass.ds(it * BODY + k, 1)].squeeze(1)


def columns(tile, it, k):
    if isinstance(it, int):
        return tile[:, (it * BODY + k) * P:(it * BODY + k + 1) * P]
    return tile[:, bass.ds(it * (BODY * P) + k * P, P)]


def block_kernel(nc, x, xT, wqk, wkv, wo, p_w, uT, w1T, w2T, b2, consts, sents, out):
    parts_dram = nc.dram_tensor("qk_parts", [3, 2, NH * DK, T], BF16, kind="Internal").ap()
    with ExitStack() as ctx:
        def sb(name, shape, dt=F32):
            return ctx.enter_context(nc.sbuf_tensor(name, shape, dt))

        def sem(name):
            return ctx.enter_context(nc.semaphore(name))

        bank = [ctx.enter_context(nc.psum_tensor(f"bank{b}", [P, 512], F32)) for b in range(8)]
        state_bank, prep_bank, out_bank = bank[0:3], bank[3:6], bank[6:8]

        x_all = sb("x_all", [P, NCH, D])
        xT_all = sb("xT_all", [D, T])
        wqk_sb = sb("wqk_sb", [D, 2 * NH * DK])
        wkv_sb = sb("wkv_sb", [D, NH * DV + NH * DK])
        wo_sb = sb("wo_sb", [P, NH * DV // P, D])
        cst = sb("cst", [P, 3 * P + 36])
        ident, mask = cst[:, 0:P], cst[:, P:2 * P]
        main_bias, rest_bias = cst[:, 3 * P + 32:3 * P + 33], cst[:, 3 * P + 33:3 * P + 34]
        one_col, eps_col = cst[:, 3 * P + 34:3 * P + 35], cst[:, 3 * P + 35:3 * P + 36]
        form_bf = sb("form_bf", [P, P + 32], BF16)
        pw_sb = sb("pw_sb", [64, D])
        uT_sb = sb("uT_sb", [64, NR * NE])
        route_w = sb("route_w", [D, P])
        b2_sb = sb("b2_sb", [P, D])
        w1_sb = sb("w1_sb", [D, NE * D])
        w2_sb = sb("w2_sb", [D, NE * D])
        sent_sb = sb("sent_sb", [P, NR, 5])

        x1_all = sb("x1_all", [P, NCH, D])
        x1T_all = sb("x1T_all", [D, T])
        z_all = sb("z_all", [P, NCH, NR, NE])
        zm_all = sb("zm_all", [P, NCH, NR, NE])
        zmax_all = sb("zmax_all", [P, NCH, NR])

        attention_room = ctx.enter_context(ExitStack())

        def asb(name, shape, dt=F32):
            return attention_room.enter_context(nc.sbuf_tensor(name, shape, dt))

        hi = asb("hi", [P, 4, GRP], BF16)
        mid = asb("mid", [P, 4, GRP], BF16)
        low = asb("low", [P, 4, GRP], BF16)
        rem = asb("rem", [P, 4, GRP])
        q_st = [asb(f"q_st{b}", [KS, NH, PAIR], BF16) for b in range(2)]
        k_st = [asb(f"k_st{b}", [KS, NH, PAIR], BF16) for b in range(2)]

        xc = asb("xc", [D, P])
        qf = asb("qf", [P, NH, P])
        qx = asb("qx", [P, NG, P])
        sq = asb("sq", [P, NH, P])
        at = asb("at", [P, NH, P])
        v1 = asb("v1", [P, NH, VW])
        k2 = asb("k2", [P, NH, 2 * NA])
        ksum = asb("ksum", [P, NH])
        kdiag = asb("kdiag", [P, NH, NA])
        kf = asb("kf", [P, NH, KFW])
        st = asb("st", [P, NH, VW])
        sx = asb("sx", [P, NG, HPG, DE])
        den = asb("den", [P, NH])
        rden = asb("rden", [P, NH])
        yn = asb("yn", [P, NH, DV])
        yT = asb("yT", [P, NH * DV // P, P])
        res = asb("res", [P, D])
        stats = asb("stats", [P, 6])
        mv = asb("mv", [P, 2])
        sd = asb("sd", [P, 1])
        rs = asb("rs", [P, 1])
        x1c = asb("x1c", [P, D])
        x1T = asb("x1T", [D, P])
        zc = asb("zc", [P, NR, ZW])
        top = asb("top", [P, NR, 8])
        zm = asb("zm", [P, NR, ZW])

        io = [sem(f"loaded_{n}") for n in ("qk_in", "kv_in", "consts", "late", "ffn", "b2")]
        in_qk, in_kv, in_cst, in_late, in_ffn, in_b2 = io
        proj_done, hi_ready, rem_ready = sem("proj_done"), sem("hi_ready"), sem("rem_ready")
        mid_ready, low_ready = sem("mid_ready"), sem("low_ready")
        stored = [sem(f"parts_stored{t}") for t in range(4)]
        stacked = [sem(f"stacked{b}") for b in range(2)]
        init_v, init_g = sem("init_vector"), sem("init_gpsimd")
        qf_done, qx_done, s_done, kv_done = sem("qf_done"), sem("qx_done"), sem("s_done"), sem("kv_done")
        y_done, st_done, yt_done, wo_done = sem("y_done"), sem("st_done"), sem("yt_done"), sem("wo_done")
        x1t_done, z_done, rw_done = sem("x1t_done"), sem("z_done"), sem("rw_done")
        qf_ready, qx_ready, sq_ready, v_ready = sem("qf_ready"), sem("qx_ready"), sem("sq_ready"), sem("v_ready")
        st_ready, yt_ready, sd_ready, x1t_ready = sem("st_ready"), sem("yt_ready"), sem("sd_ready"), sem("x1t_ready")
        at_ready, k2_ready, kd_ready, kp_ready = sem("at_ready"), sem("k2_ready"), sem("kd_ready"), sem("kp_ready")
        yn_ready, res_ready, var_ready, x1_ready = sem("yn_ready"), sem("res_ready"), sem("var_ready"), sem("x1_ready")
        z_ready, xc_ready, rw_ready = sem("z_ready"), sem("xc_ready"), sem("rw_ready")
        x1_saved, zsaved = sem("x1_saved"), sem("z_saved")
        dve_step = sem("dve_step")
        passed = sem("passed")

        x1t_saved = sem("x1t_saved")
        N_INIT_V, N_INIT_G = 4, 6

        with nc.Block() as block:
            @block.sync
            def _(sp):
                sp.dma_start(wqk_sb[:], wqk).then_inc(in_qk, 16)
                sp.dma_start(xT_all[:], xT).then_inc(in_qk, 16)
                sp.dma_start(cst[:], consts).then_inc(in_cst, 16)
                sp.dma_start(wkv_sb[:], wkv).then_inc(in_kv, 16)
                sp.dma_start(x_all[:], x.rearrange("(c p) d -> p c d", p=P)).then_inc(in_late, 16)
                sp.dma_start(wo_sb[:], wo.rearrange("(t p) d -> p t d", p=P)).then_inc(in_late, 16)
                sp.dma_start(pw_sb[:], p_w).then_inc(in_late, 16)
                sp.dma_start(uT_sb[:], uT).then_inc(in_late, 16)
                sp.dma_start(sent_sb[:], sents).then_inc(in_late, 16)
                sp.dma_start(w1_sb[:], w1T).then_inc(in_ffn, 16)
                sp.dma_start(w2_sb[:], w2T).then_inc(in_ffn, 16)
                with sp.Fori(0, T // GRP) as g:
                    for t in range(4):
                        rows = slice((t % 2) * P, (t % 2) * P + P)
                        sp.wait_ge(hi_ready, g * 4 + (t + 1))
                        sp.wait_ge(mid_ready, g * 4 + (t + 1))
                        sp.wait_ge(low_ready, g * 4 + (t + 1))
                        for part, tile in enumerate((hi, mid, low)):
                            sp.dma_start(parts_dram[part, t // 2, rows, bass.ds(g * GRP, GRP)],
                                         tile[:, t, :]).then_inc(stored[t], 16)

                def load_pair(b, p):
                    for which, (dst, parts) in enumerate(((q_st[b], Q_PARTS), (k_st[b], K_PARTS))):
                        for j, part in enumerate(parts):
                            src = parts_dram[part, which, :, bass.ds(p * PAIR, PAIR)]
                            sp.dma_start(dst[j * DK:(j + 1) * DK, :, :],
                                         src.rearrange("(h i) n -> i h n", i=DK)).then_inc(stacked[b], 16)

                for t in range(4):
                    sp.wait_ge(stored[t], 48 * (T // GRP + 1))
                load_pair(0, 0)
                load_pair(1, 1)
                with sp.Fori(0, NIT - 1) as it:
                    for b in range(2):
                        sp.wait_ge(s_done, count(it, 2 * b + 2, NG, 0))
                        load_pair(b, it * 2 + (2 + b))

            @block.tensor
            def _(pe):
                pe.wait_ge(in_qk, 32)
                with pe.Fori(0, T // GRP) as g:
                    for t in range(4):
                        pe.wait_ge(rem_ready, g * 4 + (t + 1))
                        nc.tensor.matmul(bank[t][:], wqk_sb[:, t * P:(t + 1) * P], xT_all[:, bass.ds(g * GRP, GRP)],
                                         start=True, stop=True).then_inc(proj_done, 1)
                pe.wait_ge(in_late, 16 * 5)
                pe.wait_ge(init_v, N_INIT_V)
                nc.tensor.matmul(out_bank[0][:, 0:NR * NE], pw_sb[:], uT_sb[:], start=True, stop=True).then_inc(rw_done, 1)
                pe.wait_ge(init_g, N_INIT_G)
                pe.wait_ge(rem_ready, 4 * (T // GRP) + 4)
                st_flat, sx_flat = st[:].rearrange("p h e -> p (h e)"), sx[:].rearrange("p g j e -> p (g j e)")
                for b in range(3):
                    nc.tensor.matmul(state_bank[b][:], st_flat[:, 0:P], sx_flat[:, 0:512], start=True, stop=True)
                pe.wait_ge(rw_ready, 1)

                def query_features(it, k, g):
                    b, off = (k // 2) % 2, (k % 2) * P
                    nc.tensor.matmul(prep_bank[g % 3][:], form_bf[0:KS, 0:P],
                                     q_st[b][:, HPG * g:HPG * g + HPG, off:off + P],
                                     start=True, stop=True).then_inc(qf_done, 1)

                def query_rest(it, k):
                    b, off = (k // 2) % 2, (k % 2) * P
                    for j in range(HPG):
                        mm = nc.tensor.matmul(prep_bank[1][32 * j:32 * j + 32, :], form_bf[0:KS, P:P + 32],
                                              q_st[b][:, j:NH:HPG, off:off + P], start=True, stop=True)
                    mm.then_inc(qx_done, 1)

                def scores(it, k, g):
                    b, off = (k // 2) % 2, (k % 2) * P
                    for j in range(HPG):
                        h = HPG * g + j
                        mm = nc.tensor.matmul(prep_bank[(5 + g) % 3][:, j * P:(j + 1) * P],
                                              k_st[b][:, h, off:off + P], q_st[b][:, h, off:off + P],
                                              start=True, stop=True)
                    mm.then_inc(s_done, 1)

                def keys_values(it, k, u):
                    n = 512 if u < 2 else NH * DK
                    nc.tensor.matmul(prep_bank[u][:, 0:n], xc[:], wkv_sb[:, u * 512:u * 512 + n],
                                     start=True, stop=True).then_inc(kv_done, 1)

                def prep_group(it, k, g):
                    if g == 0:
                        pe.wait_ge(v_ready, count(it, k, 2, 1))
                        if k % 2 == 0:
                            pe.wait_ge(stacked[(k // 2) % 2], (it + (k // BODY + 1)) * (2 * NPIECE * 16))
                    if g == 1:
                        pe.wait_ge(v_ready, count(it, k, 2, 2))
                    if g == 2:
                        pe.wait_ge(k2_ready, count(it, k, 1, 1))
                    if g == 3:
                        pe.wait_ge(qf_ready, count(it, k, NG, 1))
                    query_features(it, k, g)

                def prep_rest(it, k):
                    pe.wait_ge(qf_ready, count(it, k, NG, 2))
                    query_rest(it, k)

                def prep_scores(it, k, g):
                    if g < 2:
                        pe.wait_ge(qf_ready, count(it, k, NG, 3 + g))
                    elif g == 2:
                        pe.wait_ge(qx_ready, count(it, k, 1, 1))
                    else:
                        pe.wait_ge(sq_ready, count(it, k, NG, 1))
                    scores(it, k, g)

                def prep_kv(it, k, u):
                    pe.wait_ge(sq_ready, count(it, k, NG, 2 + u))
                    if u == 0:
                        pe.wait_ge(in_kv, 16)
                        pe.wait_ge(xc_ready, count(it, k, 1, 1))
                    keys_values(it, k, u)

                def attend(it, k, g):
                    ob = out_bank[(9 * k + g) % 2]
                    if g == 0:
                        pe.wait_ge(x1t_ready, count(it, k, 1, 1))
                        pe.wait_ge(st_ready, count(it, k, 1, 1))
                        pe.wait_ge(qx_ready, count(it, k, 1, 1))
                        pe.wait_ge(v_ready, count(it, k, 2, 4))
                    elif g == 1:
                        pe.wait_ge(z_ready, count(it, k, 1, 1))
                    else:
                        pe.wait_ge(yn_ready, count(it, k, NG, g - 1))
                    pe.wait_ge(qf_ready, count(it, k, NG, g + 1))
                    pe.wait_ge(at_ready, count(it, k, NG, g + 1))
                    nc.tensor.matmul(ob[:, 0:HPG * DE], qx[:, g, :], sx[:, g, :, :].rearrange("p a b -> p (a b)"),
                                     start=True, stop=False, skip_group_check=True)
                    for j in range(HPG):
                        h = HPG * g + j
                        o = ob[:, j * DE:j * DE + VW]
                        nc.tensor.matmul(o, qf[:, h, :], st[:, h, :], start=False, stop=False, skip_group_check=True)
                        mm = nc.tensor.matmul(o, at[:, h, :], v1[:, h, :], start=False, stop=(j == HPG - 1),
                                              skip_group_check=True)
                    mm.then_inc(y_done, 1)

                def grow_state(it, k, heads):
                    if heads[0] == 0:
                        pe.wait_ge(kd_ready, count(it, k, 1, 1))
                        pe.wait_ge(kp_ready, count(it, k, 1, 2))
                    for h in heads:
                        o = state_bank[h // HPB][:, (h % HPB) * DE:(h % HPB) * DE + VW]
                        mm = nc.tensor.matmul(o, kf[:, h, 0:P], v1[:, h, :], start=False, stop=True,
                                              skip_group_check=True)
                        if h == HPB - 1:
                            mm.then_inc(st_done, 1)
                    if heads[-1] == NH - 1:
                        for h in range(NH):
                            g, j = h // HPG, h % HPG
                            o = state_bank[2][32 * j:32 * j + 32, (2 + g) * DE:(2 + g) * DE + VW]
                            mm = nc.tensor.matmul(o, kf[:, h, P:KFW], v1[:, h, :], start=False, stop=True,
                                                  skip_group_check=True)
                        mm.then_inc(st_done, 1)

                def turn_y(it, k, u):
                    ob = out_bank[(9 * k + 4 + u) % 2]
                    pe.wait_ge(yn_ready, count(it, k, NG, 4 if u else 3))
                    for j in range(4):
                        y2 = yn[:].rearrange("p h e -> p (h e)")
                        mm = nc.tensor.transpose(ob[:, j * P:(j + 1) * P], y2[:, (4 * u + j) * P:(4 * u + j + 1) * P], ident)
                    mm.then_inc(yt_done, 1)

                def project_y(it, k):
                    ob = out_bank[(9 * k + 6) % 2]
                    pe.wait_ge(yt_ready, count(it, k, 2, 2))
                    for j in range(8):
                        mm = nc.tensor.matmul(ob[:, 0:D], yT[:, j, :], wo_sb[:, j, :], start=(j == 0), stop=(j == 7))
                    mm.then_inc(wo_done, 1)

                def turn_x1(it, k):
                    ob = out_bank[(9 * k + 7) % 2]
                    pe.wait_ge(x1_ready, count(it, k, 1, 1))
                    nc.tensor.transpose(ob[:, 0:P], x1c[:], ident).then_inc(x1t_done, 1)

                def route(it, k):
                    ob = out_bank[(9 * k + 8) % 2]
                    pe.wait_ge(x1t_ready, count(it, k, 1, 2))
                    nc.tensor.matmul(ob[:, 0:P], x1T[:], route_w[:], start=True, stop=True).then_inc(z_done, 1)

                def chunk(it, k, last=False):
                    n = k + 1
                    for g in range(NG):
                        attend(it, k, g)
                        if not last:
                            prep_group(it, n, g)
                    grow_state(it, k, range(0, 8))
                    if not last:
                        prep_rest(it, n)
                        prep_scores(it, n, 0)
                        prep_scores(it, n, 1)
                    turn_y(it, k, 0)
                    turn_y(it, k, 1)
                    grow_state(it, k, range(8, NH))
                    if not last:
                        prep_scores(it, n, 2)
                        prep_scores(it, n, 3)
                    project_y(it, k)
                    if not last:
                        prep_kv(it, n, 0)
                        prep_kv(it, n, 1)
                    turn_x1(it, k)
                    if not last:
                        prep_kv(it, n, 2)
                    route(it, k)

                for g in range(NG):
                    prep_group(0, 0, g)
                prep_rest(0, 0)
                for g in range(NG):
                    prep_scores(0, 0, g)
                for u in range(3):
                    prep_kv(0, 0, u)
                with pe.Fori(0, NIT - 1) as it:
                    for k in range(BODY):
                        chunk(it, k)
                for k in range(BODY):
                    chunk(NIT - 1, k, last=(k == BODY - 1))

            @block.scalar
            def _(act):
                def part(t, dst, src, ready):
                    nc.scalar.activation(dst[:, t, :], src, ACT.Copy).then_inc(ready, 1)

                act.sem_inc(st_ready, 1)
                act.sem_inc(v_ready, 2)
                act.sem_inc(x1t_ready, 1)
                for t in range(4):
                    act.sem_inc(stored[t], 48)
                with act.Fori(0, T // GRP) as g:
                    def high(t):
                        act.wait_ge(proj_done, g * 4 + (t + 1))
                        act.wait_ge(stored[t], (g + 1) * 48)
                        part(t, hi, bank[t][:], hi_ready)

                    def middle(t):
                        act.wait_ge(rem_ready, g * 4 + (t + 5))
                        part(t, mid, rem[:, t, :], mid_ready)

                    high(0)
                    for t in range(1, 4):
                        high(t)
                        middle(t - 1)
                    middle(3)
                act.wait_ge(in_cst, 16)

                def query_squares(it, k, g):
                    act.wait_ge(qf_done, count(it, k, NG, g + 1))
                    nc.scalar.activation(qf[:, HPG * g:HPG * g + HPG, :], prep_bank[g % 3][:].rearrange("p (h n) -> p h n", h=HPG),
                                         ACT.Square, bias=main_bias).then_inc(qf_ready, 1)

                def rest_squares(it, k):
                    act.wait_ge(qx_done, count(it, k, 1, 1))
                    nc.scalar.activation(qx[:], prep_bank[1][:].rearrange("p (g n) -> p g n", g=NG),
                                         ACT.Square, bias=rest_bias).then_inc(qx_ready, 1)

                def score_squares(it, k, g, first=False):
                    act.wait_ge(s_done, count(it, k, NG, g + 1))
                    if not first:
                        act.wait_ge(at_ready, count(it, k, NG, g - 3))
                    nc.scalar.activation(sq[:, HPG * g:HPG * g + HPG, :], prep_bank[(5 + g) % 3][:].rearrange("p (h n) -> p h n", h=HPG),
                                         ACT.Square, bias=one_col, scale=0.25).then_inc(sq_ready, 1)

                def take_values(it, k, u):
                    act.wait_ge(kv_done, count(it, k, 3, u + 1))
                    nc.scalar.activation(v1[:, 8 * u:8 * u + 8, 0:DV], prep_bank[u][:].rearrange("p (h e) -> p h e", e=DV),
                                         ACT.Copy).then_inc(v_ready, 1)

                def take_state(it, k, half):
                    act.wait_ge(st_done, count(it, k, 2, half + 1))
                    for b in ((0,), (1, 2))[half]:
                        n = min(HPB, NH - HPB * b)
                        nc.scalar.activation(st[:, HPB * b:HPB * b + n, 0:DE],
                                             state_bank[b][:, 0:n * DE].rearrange("p (h e) -> p h e", e=DE), ACT.Copy)
                    if half:
                        for j in range(HPG):
                            rows = slice(32 * j, 32 * j + 32)
                            last = nc.scalar.activation(sx[rows, :, j, :],
                                                        state_bank[2][rows, 2 * DE:(2 + NG) * DE].rearrange("p (g e) -> p g e", e=DE),
                                                        ACT.Copy)
                        last.then_inc(st_ready, 1)

                def take_turned_y(it, k, u):
                    act.wait_ge(yt_done, count(it, k, 2, u + 1))
                    nc.scalar.activation(yT[:, 4 * u:4 * u + 4, :],
                                         out_bank[(9 * k + 4 + u) % 2][:].rearrange("p (j n) -> p j n", j=4),
                                         ACT.Copy).then_inc(yt_ready, 1)

                def deviation(it, k):
                    act.wait_ge(var_ready, count(it, k, 1, 1))
                    nc.scalar.activation(sd[:], mv[:, 1:2], ACT.Sqrt, bias=eps_col).then_inc(sd_ready, 1)

                def take_turned_x1(it, k):
                    act.wait_ge(x1t_done, count(it, k, 1, 1))
                    act.wait_ge(x1t_saved, count(it, k, 1, 1))
                    nc.scalar.activation(x1T[:], out_bank[(9 * k + 7) % 2][:, 0:P], ACT.Copy).then_inc(x1t_ready, 1)

                def chunk(it, k, last=False):
                    n = k + 1
                    if not last:
                        for g in range(NG):
                            query_squares(it, n, g)
                    if not last:
                        take_state(it, k, 0)
                        rest_squares(it, n)
                        score_squares(it, n, 0)
                        score_squares(it, n, 1)
                    take_turned_y(it, k, 0)
                    take_turned_y(it, k, 1)
                    if not last:
                        score_squares(it, n, 2)
                        score_squares(it, n, 3)
                        take_state(it, k, 1)
                    deviation(it, k)
                    if not last:
                        take_values(it, n, 0)
                        take_values(it, n, 1)
                    take_turned_x1(it, k)

                for g in range(NG):
                    query_squares(0, 0, g)
                rest_squares(0, 0)
                for g in range(NG):
                    score_squares(0, 0, g, first=True)
                take_values(0, 0, 0)
                take_values(0, 0, 1)
                with act.Fori(0, NIT - 1) as it:
                    for k in range(BODY):
                        chunk(it, k)
                for k in range(BODY):
                    chunk(NIT - 1, k, last=(k == BODY - 1))

            @block.vector
            def _(dve):
                dve.sem_inc(rem_ready, 4)
                dve.sem_inc(k2_ready, 1)
                dve.sem_inc(z_ready, 1)
                dve.wait_ge(in_cst, 16)
                nc.vector.tensor_copy(form_bf[:], cst[:, 2 * P:3 * P + 32]).then_inc(init_v, 1)
                nc.vector.memset(route_w[:], 0.0).then_inc(init_v, 1)
                nc.vector.memset(k2[:, :, DK:2 * NA:NA], 1.0).then_inc(init_v, 1)
                with dve.Fori(0, T // GRP) as g:
                    def remainder(t):
                        dve.wait_ge(hi_ready, g * 4 + (t + 1))
                        nc.vector.tensor_tensor(rem[:, t, :], bank[t][:], hi[:, t, :], ALU.subtract).then_inc(rem_ready, 1)

                    def lowest(t):
                        dve.wait_ge(mid_ready, g * 4 + (t + 1))
                        nc.vector.tensor_tensor(low[:, t, :], rem[:, t, :], mid[:, t, :], ALU.subtract).then_inc(low_ready, 1)

                    remainder(0)
                    for t in range(1, 4):
                        remainder(t)
                        lowest(t - 1)
                    lowest(3)
                dve.wait_ge(in_late, 16 * 5)
                nc.vector.tensor_copy(zc[:, :, NE:ZW], sent_sb[:]).then_inc(init_v, 1)
                dve.wait_ge(rw_done, 1)
                dve.wait_ge(init_v, N_INIT_V)
                nc.vector.tensor_copy(route_w[:, 0:NR * NE], out_bank[0][:, 0:NR * NE]).then_inc(rw_ready, 1)

                BEFORE, PER = 3, 17
                at_chunk = [0, 0, -BEFORE]

                def step(ins):
                    it, k, done = at_chunk
                    ins.then_inc(dve_step, 1)
                    at_chunk[2] = done + 1
                    dve.wait_ge(dve_step, count(it, k, PER, BEFORE + done + 1))

                def normalize(it, k, g):
                    ob = out_bank[(9 * k + g) % 2][:, 0:HPG * DE].rearrange("p (h e) -> p h e", e=DE)
                    heads = slice(HPG * g, HPG * g + HPG)
                    dve.wait_ge(y_done, count(it, k, NG, g + 1))
                    step(nc.vector.tensor_scalar(den[:, heads], ob[:, :, DV], 2 * EPS_Z, None, ALU.add))
                    step(nc.vector.reciprocal(rden[:, heads], den[:, heads]))
                    nc.vector.tensor_tensor(yn[:, heads, :], ob[:, :, 0:DV],
                                            rden[:, heads].unsqueeze(2).broadcast_to([P, HPG, DV]),
                                            ALU.mult).then_inc(yn_ready, 1)

                def mask_scores(it, k, g):
                    heads = slice(HPG * g, HPG * g + HPG)
                    dve.wait_ge(sq_ready, count(it, k, NG, g + 1))
                    nc.vector.scalar_tensor_tensor(out=at[:, heads, :], in0=sq[:, heads, :], scalar=1.0,
                                                   in1=mask.unsqueeze(1).broadcast_to([P, HPG, P]),
                                                   op0=ALU.add, op1=ALU.mult).then_inc(at_ready, 1)

                def take_keys(it, k):
                    kb = prep_bank[2][:, 0:NH * DK].rearrange("p (h i) -> p h i", i=DK)
                    dve.wait_ge(kv_done, count(it, k, 3, 3))
                    dve.wait_ge(kp_ready, count(it, k, 1, 1))
                    nc.vector.tensor_copy(k2[:, :, 0:DK], kb)
                    nc.vector.tensor_copy(k2[:, :, NA:NA + DK], kb).then_inc(k2_ready, 1)

                def key_diagonal(it, k):
                    dve.wait_ge(k2_ready, count(it, k, 1, 2))
                    step(nc.vector.reduce_sum(ksum[:], k2[:, :, 0:NA], AX_X))
                    step(nc.vector.scalar_tensor_tensor(out=kdiag[:], in0=k2[:, :, 0:NA], scalar=2.0,
                                                               in1=ksum[:].unsqueeze(2).broadcast_to([P, NH, NA]),
                                                               op0=ALU.mult, op1=ALU.subtract))
                    step(nc.vector.tensor_tensor(kf[:, :, 0:NA], kdiag[:], k2[:, :, 0:NA], ALU.mult))
                    nc.vector.tensor_scalar(kf[:, :, DK], kf[:, :, DK], 1.0, None, ALU.add).then_inc(kd_ready, 1)

                def add_residual(it, k):
                    dve.wait_ge(wo_done, count(it, k, 1, 1))
                    step(nc.vector.tensor_tensor(res[:], out_bank[(9 * k + 6) % 2][:, 0:D],
                                                        row(x_all, it, k), ALU.add))
                    step(nc.vector.bn_stats(stats[:], res[:]))
                    dve.sem_inc(passed, 1)
                    nc.vector.bn_aggr(mv[:], stats[:]).then_inc(var_ready, 1)

                def norm(it, k):
                    dve.wait_ge(sd_ready, count(it, k, 1, 1))
                    step(nc.vector.reciprocal(rs[:], sd[:]))
                    dve.wait_ge(x1_saved, count(it, k, 1, 1))
                    nc.vector.tensor_scalar(x1c[:], res[:], mv[:, 0:1], rs[:], ALU.subtract, ALU.mult).then_inc(x1_ready, 1)

                def take_routes(it, k):
                    dve.wait_ge(z_done, count(it, k, 1, 1))
                    nc.vector.tensor_copy(zc[:, :, 0:NE], out_bank[(9 * k + 8) % 2][:, 0:NR * NE].rearrange("p (r e) -> p r e", e=NE))\
                      .then_inc(z_ready, 1)

                def choose(it, k):
                    dve.wait_ge(z_ready, count(it, k, 1, 2))
                    dve.sem_inc(passed, 1)
                    for r in range(NR):
                        mx = nc.vector.max(out=top[:, r, :], in_=zc[:, r, 0:NE])
                    step(mx)
                    nc.vector.tensor_copy(row(zmax_all, it, k), top[:, :, 0])
                    step(nc.vector.tensor_copy(top[:, :, TOPK:8], sent_sb[:]))
                    dve.sem_inc(passed, 1)
                    for r in range(NR):
                        mr = nc.vector.match_replace(out=zm[:, r, :], in_to_replace=top[:, r, :], in_values=zc[:, r, :], imm_value=SENT)
                    step(mr)
                    nc.vector.tensor_copy(row(z_all, it, k), zc[:, :, 0:NE])
                    nc.vector.tensor_copy(row(zm_all, it, k), zm[:, :, 0:NE]).then_inc(zsaved, 1)

                def chunk(it, k, last=False):
                    n = k + 1
                    at_chunk[:] = [it, k, 0]
                    for g in range(NG):
                        normalize(it, k, g)
                    if not last:
                        for g in range(NG):
                            mask_scores(it, n, g)
                    add_residual(it, k)
                    norm(it, k)
                    if not last:
                        take_keys(it, n)
                    take_routes(it, k)
                    choose(it, k)
                    if not last:
                        key_diagonal(it, n)
                        assert at_chunk[2] == PER

                for g in range(NG):
                    mask_scores(0, 0, g)
                take_keys(0, 0)
                key_diagonal(0, 0)
                with dve.Fori(0, NIT - 1) as it:
                    for k in range(BODY):
                        chunk(it, k)
                for k in range(BODY):
                    chunk(NIT - 1, k, last=(k == BODY - 1))

            @block.gpsimd
            def _(pool):
                nc.gpsimd.memset(st[:], 0.0).then_inc(init_g, 1)
                nc.gpsimd.memset(sx[:], 0.0).then_inc(init_g, 1)
                nc.gpsimd.memset(v1[:], 0.0).then_inc(init_g, 1)
                nc.gpsimd.memset(kf[:], 0.0).then_inc(init_g, 1)
                nc.gpsimd.memset(b2_sb[:], 0.0).then_inc(init_g, 1)
                pool.wait_ge(init_g, N_INIT_G - 1)
                nc.gpsimd.memset(v1[:, :, DV], 1.0).then_inc(init_g, 1)
                pool.sem_inc(kp_ready, 1)
                pool.sem_inc(x1_saved, 1)
                pool.sem_inc(x1t_saved, 1)
                pool.wait_ge(init_g, N_INIT_G)
                pool.dma_start(b2_sb[2 * NE:3 * NE, :], b2).then_inc(in_b2, 16)

                def take_x(it, k, first=False):
                    if not first:
                        pool.wait_ge(kv_done, count(it, k, 3, 0))
                    nc.gpsimd.tensor_copy(xc[:], columns(xT_all, it, k)).then_inc(xc_ready, 1)

                def key_products(it, k):
                    pool.wait_ge(k2_ready, count(it, k, 1, 2))
                    whole = k2[:]
                    ahead = bass.AP(whole.tensor, whole.offset + 1,
                                    [whole.ap[0], (2 * NA, NH), (1, NF // NA - 1), (1, NA)])
                    here = k2[:, :, 0:NA].unsqueeze(2).broadcast_to([P, NH, NF // NA - 1, NA])
                    out4 = kf[:, :, NA:NF].rearrange("p h (d i) -> p h d i", i=NA)
                    nc.gpsimd.tensor_tensor(out4, here, ahead, ALU.mult).then_inc(kp_ready, 1)

                def keep_x1(it, k):
                    pool.wait_ge(x1_ready, count(it, k, 1, 1))
                    nc.gpsimd.tensor_copy(row(x1_all, it, k), x1c[:]).then_inc(x1_saved, 1)
                    pool.wait_ge(x1t_ready, count(it, k, 1, 2))
                    nc.gpsimd.tensor_copy(columns(x1T_all, it, k), x1T[:]).then_inc(x1t_saved, 1)

                pool.wait_ge(in_qk, 32)
                take_x(0, 0, first=True)
                pool.wait_ge(init_v, 3)
                key_products(0, 0)
                with pool.Fori(0, NIT - 1) as it:
                    for k in range(BODY):
                        take_x(it, k + 1)
                        keep_x1(it, k)
                        key_products(it, k + 1)
                for k in range(BODY):
                    if k < BODY - 1:
                        take_x(NIT - 1, k + 1)
                    keep_x1(NIT - 1, k)
                    if k < BODY - 1:
                        key_products(NIT - 1, k + 1)

        attention_room.close()
        ex = sb("ex", [P, NCH * NR, NE])
        wsum = sb("wsum", [P, NCH * NR])
        wr = sb("wr", [P, NCH * NR])
        mix_all = sb("mix_all", [P, NCH, NR, NE])
        xb = [sb(f"xb{b}", [D, P]) for b in range(BODY)]
        cw = [sb(f"cw{b}", [P, P]) for b in range(BODY)]
        acc1, acc2 = sb("acc1", [P, 2, D]), sb("acc2", [P, 2, D])
        prod1, prod2 = sb("prod1", [P, EU, D]), sb("prod2", [P, EU + 1, D])
        half1, half2 = sb("half1", [P, 2, D]), sb("half2", [P, 2, D])
        rest1, rest2, rest3 = sb("rest1", [P, D]), sb("rest2", [P, D]), sb("rest3", [P, D])
        pair1, pair2 = sb("pair1", [P, D]), sb("pair2", [P, D])
        hsum = [sb(f"hsum{b}", [P, D]) for b in range(2)]
        hh = [sb(f"hh{b}", [P, D]) for b in range(2)]
        hT = sb("hT", [P, P])
        cT = sb("cT", [P, P])
        ysum = sb("ysum", [P, BODY, D])
        ostats, omv = sb("ostats", [P, 6]), sb("omv", [P, BODY, 2])
        osd, ors = sb("osd", [P, BODY]), sb("ors", [P, BODY])
        oc = [sb(f"oc{b}", [P, D]) for b in range(BODY)]

        cw_init, mix_step, sh_ready, ex_ready, mix_ready = (sem(n) for n in ("cw_init", "mix_step", "sh_ready", "ex_ready", "mix_ready"))
        xb_ready, l1_done, l2_done, turned, took = (sem(n) for n in ("xb_ready", "l1_done", "l2_done", "turned", "took"))
        b2_done, mixed1, mixed2, prod1_ready, prod2_ready = (sem(n) for n in ("b2_done", "mixed1", "mixed2", "prod1_ready", "prod2_ready"))
        hsum_ready, h_ready, half1_ready, half2_ready = (sem(n) for n in ("hsum_ready", "h_ready", "half1_ready", "half2_ready"))
        sum_step, rest3_ready, pair2_ready = (sem(n) for n in ("sum_step", "rest3_ready", "pair2_ready"))
        ysum_ready, ovar_ready, osd_ready, ors_ready, oc_ready, ostep = (sem(n) for n in ("ysum_ready", "ovar_ready", "osd_ready", "ors_ready", "oc_ready", "ostep"))
        out_saved = [sem(f"out_saved{b}") for b in range(BODY)]
        DVE_E = 2 * EU

        with nc.Block() as block:
            @block.sync
            def _(sp):
                for k in range(BODY):
                    sp.sem_inc(out_saved[k], 16)
                with sp.Fori(0, NIT) as it:
                    for k in range(BODY):
                        sp.wait_ge(oc_ready, count(it, k, 1, 1))
                        sp.dma_start(out[bass.ds(it * (BODY * P) + k * P, P), :], oc[k][:]).then_inc(out_saved[k], 16)
                for k in range(BODY):
                    sp.wait_ge(out_saved[k], 16 * (NIT + 1))

            @block.gpsimd
            def _(pool):
                for b in range(BODY):
                    nc.gpsimd.memset(cw[b][:], 0.0).then_inc(cw_init, 1)
                pool.sem_inc(half1_ready, 1)
                pool.sem_inc(rest3_ready, 1)
                pool.wait_ge(cw_init, BODY)
                at_chunk = [0, 0, 0]

                def step(ins):
                    it, k, n = at_chunk
                    ins.then_inc(sum_step, 1)
                    at_chunk[2] = n + 1
                    pool.wait_ge(sum_step, BEFORE + count(it, k, PER, n + 1) if it is not None else n + 1)

                PER, BEFORE = 4, 4

                def stage(it, k, first=False):
                    if not first:
                        pool.wait_ge(mixed2, count(it, k, DVE_E, -2 * DVE_E))
                        pool.wait_ge(prod2_ready, count(it, k, 1, -2))
                    nc.gpsimd.tensor_copy(xb[k % BODY][:], columns(x1T_all, it, k)).then_inc(xb_ready, 1)
                    if first and k == 0:
                        pool.wait_ge(mix_ready, 1)
                    nc.gpsimd.tensor_copy(cw[k % BODY][:, 0:NR * NE], row(mix_all, it, k).rearrange("p r e -> p (r e)"))\
                      .then_inc(xb_ready, 1)

                def hidden_sum(it, k, first=False):
                    pool.wait_ge(prod1_ready, count(it, k, 1, 2))
                    step(nc.gpsimd.tensor_tensor(half1[:], prod1[:, 0:2, :], prod1[:, 2:4, :], ALU.add))
                    nc.gpsimd.tensor_tensor(rest1[:], half1[:, 0, :], half1[:, 1, :], ALU.add).then_inc(half1_ready, 1)
                    pool.wait_ge(mixed1, count(it, k, DVE_E, 2 * DVE_E))
                    step(nc.gpsimd.tensor_tensor(pair1[:], acc1[:, 0, :], acc1[:, 1, :], ALU.add))
                    pool.wait_ge(half1_ready, count(it, k, 1, 2))
                    if not first:
                        pool.wait_ge(h_ready, count(it, k, 1, -1))
                    nc.gpsimd.tensor_tensor(hsum[k % 2][:], pair1[:], rest1[:], ALU.add).then_inc(hsum_ready, 1)

                def output_rest(it, k):
                    pool.wait_ge(prod2_ready, count(it, k, 1, 2))
                    step(nc.gpsimd.tensor_tensor(half2[:], prod2[:, 0:2, :], prod2[:, 2:4, :], ALU.add))
                    step(nc.gpsimd.tensor_tensor(rest2[:], half2[:, 0, :], half2[:, 1, :], ALU.add))
                    pool.wait_ge(ysum_ready, count(it, k, 1, 1))
                    nc.gpsimd.tensor_tensor(rest3[:], rest2[:], prod2[:, EU, :], ALU.add).then_inc(rest3_ready, 1)

                for k in range(BODY):
                    stage(0, k, first=True)
                for k in range(2):
                    at_chunk[:] = [None, 0, 2 * k]
                    hidden_sum(0, k, first=True)
                with pool.Fori(0, NIT - 1) as it:
                    for k in range(BODY):
                        at_chunk[:] = [it, k, 0]
                        output_rest(it, k)
                        stage(it, k + BODY)
                        hidden_sum(it, k + 2)
                        assert at_chunk[2] == PER
                for k in range(BODY):
                    at_chunk[:] = [NIT - 1, k, 0 if k < BODY - 1 else -2]
                    output_rest(NIT - 1, k)
                    if k + 2 < BODY:
                        hidden_sum(NIT - 1, k + 2)

            @block.tensor
            def _(pe):
                def first(it, k):
                    pe.wait_ge(xb_ready, count(it, k, 2, 1))
                    for u in (2, 0, 1):
                        if u == 2:
                            pe.wait_ge(prod1_ready, count(it, k, 1, 1))
                        else:
                            pe.wait_ge(mixed1, count(it, k, DVE_E, EU * (u + 1)))
                        nc.tensor.matmul(bank[u][:], xb[k % BODY][:], w1_sb[:, u * 512:(u + 1) * 512],
                                         start=True, stop=True).then_inc(l1_done, 1)

                def turn(it, k):
                    pe.wait_ge(took, count(it, k, 2, 2))
                    pe.wait_ge(h_ready, count(it, k, 1, 1))
                    pe.wait_ge(xb_ready, count(it, k, 2, 2))
                    nc.tensor.transpose(bank[6][:, 0:P], hh[k % 2][:], ident)
                    nc.tensor.transpose(bank[6][:, P:2 * P], cw[k % BODY][:], ident).then_inc(turned, 1)

                def second(it, k):
                    pe.wait_ge(took, count(it, k, 2, 4))
                    pe.wait_ge(prod2_ready, count(it, k, 1, 1))
                    nc.tensor.matmul(bank[7][:, 0:D], cT[:], b2_sb[:], start=True, stop=True)
                    for u in (2, 0, 1):
                        if u < 2:
                            pe.wait_ge(mixed2, count(it, k, DVE_E, EU * (u + 1)))
                        nc.tensor.matmul(bank[3 + u][:], hT[:], w2_sb[:, u * 512:(u + 1) * 512],
                                         start=True, stop=True).then_inc(l2_done, 1)

                pe.wait_ge(in_ffn, 32)
                pe.wait_ge(in_b2, 16)
                for k in range(3):
                    first(0, k)
                turn(0, 0)
                second(0, 0)
                with pe.Fori(0, NIT - 1) as it:
                    for k in range(BODY):
                        turn(it, k + 1)
                        second(it, k + 1)
                        first(it, k + 3)
                for k in range(BODY):
                    if k + 1 < BODY:
                        turn(NIT - 1, k + 1)
                        second(NIT - 1, k + 1)
                    if k + 3 < BODY:
                        first(NIT - 1, k + 3)

            @block.scalar
            def _(act):
                act.sem_inc(took, 2)
                act.sem_inc(prod1_ready, 1)
                act.sem_inc(prod2_ready, 1)
                act.wait_ge(sh_ready, 1)
                nc.scalar.activation(ex[:], ex[:], ACT.Exp).then_inc(ex_ready, 1)

                def weigh(it, k, r, b, dst):
                    for j in range(EU):
                        e = (r * NE) + 2 * EU + j
                        last = nc.scalar.activation(dst[:, j, :], bank[b][:, j * D:(j + 1) * D], ACT.Copy,
                                                    scale=cw[k % BODY][:, e:e + 1])
                    return last

                def hidden_products(it, k):
                    act.wait_ge(xb_ready, count(it, k, 2, 2))
                    act.wait_ge(l1_done, count(it, k, NU, 1))
                    act.wait_ge(half1_ready, count(it, k, 1, 1))
                    weigh(it, k, 0, 2, prod1).then_inc(prod1_ready, 1)

                def output_products(it, k):
                    act.wait_ge(l2_done, count(it, k, NU, 1))
                    act.wait_ge(rest3_ready, count(it, k, 1, 1))
                    nc.scalar.activation(prod2[:, EU, :], bank[7][:, 0:D], ACT.Copy)
                    weigh(it, k, 1, 5, prod2).then_inc(prod2_ready, 1)

                def gelu(it, k):
                    act.wait_ge(hsum_ready, count(it, k, 1, 1))
                    nc.scalar.activation(hh[k % 2][:], hsum[k % 2][:], ACT.Gelu).then_inc(h_ready, 1)

                def take(it, k):
                    act.wait_ge(turned, count(it, k, 1, 1))
                    nc.scalar.activation(hT[:], bank[6][:, 0:P], ACT.Copy).then_inc(took, 1)
                    nc.scalar.activation(cT[:], bank[6][:, P:2 * P], ACT.Copy).then_inc(took, 1)

                def deviations(it):
                    act.wait_ge(ovar_ready, it * BODY + BODY)
                    nc.scalar.activation(osd[:], omv[:, :, 1], ACT.Sqrt, bias=eps_col).then_inc(osd_ready, 1)

                def chunk(it, k, left):
                    output_products(it, k)
                    if left >= 1:
                        take(it, k + 1)
                    if left >= 2:
                        hidden_products(it, k + 2)
                    if k == BODY - 1:
                        deviations(it)
                    if left >= 2:
                        gelu(it, k + 2)

                for k in range(2):
                    hidden_products(0, k)
                gelu(0, 0)
                gelu(0, 1)
                take(0, 0)
                with act.Fori(0, NIT - 1) as it:
                    for k in range(BODY):
                        chunk(it, k, BODY)
                for k in range(BODY):
                    chunk(NIT - 1, k, BODY - 1 - k)

            @block.vector
            def _(dve):
                dve.sem_inc(mixed1, DVE_E)
                dve.sem_inc(mixed2, DVE_E)
                dve.sem_inc(ysum_ready, 1)
                done = [0]

                def link(ins):
                    done[0] += 1
                    ins.then_inc(mix_step, 1)
                    dve.wait_ge(mix_step, done[0])

                z3 = z_all[:].rearrange("p c r e -> p (c r) e")
                zm3 = zm_all[:].rearrange("p c r e -> p (c r) e")
                mix3 = mix_all[:].rearrange("p c r e -> p (c r) e")
                zmax3 = zmax_all[:].rearrange("p c r -> p (c r)")
                wide = [P, NCH * NR, NE]
                nc.vector.tensor_tensor(ex[:], z3, zmax3.unsqueeze(2).broadcast_to(wide), ALU.subtract).then_inc(sh_ready, 1)
                dve.wait_ge(ex_ready, 1)
                link(nc.vector.scalar_tensor_tensor(out=mix3, in0=zm3, scalar=SENT, in1=ex[:], op0=ALU.is_equal, op1=ALU.mult))
                link(nc.vector.reduce_sum(wsum[:], mix3, AX_X))
                link(nc.vector.reciprocal(wr[:], wsum[:]))
                nc.vector.tensor_tensor(mix3, mix3, wr[:].unsqueeze(2).broadcast_to(wide), ALU.mult).then_inc(mix_ready, 1)

                def mixture(it, k, r, banks, done_sem, acc, mixed, seed=None):
                    dve.wait_ge(xb_ready, count(it, k, 2, 2))
                    for e in range(DVE_E):
                        if e % EU == 0:
                            dve.wait_ge(done_sem, count(it, k, NU, e // EU + 2))
                        src = banks[e // EU][:, (e % EU) * D:(e % EU + 1) * D]
                        a, w = acc[:, e % 2, :], cw[k % BODY][:, r * NE + e:r * NE + e + 1]
                        if e >= 2:
                            dve.wait_ge(mixed, count(it, k, DVE_E, DVE_E + e - 1))
                            ins = nc.vector.scalar_tensor_tensor(out=a, in0=src, scalar=w, in1=a, op0=ALU.mult, op1=ALU.add)
                        elif e == 0 and seed is not None:
                            ins = nc.vector.scalar_tensor_tensor(out=a, in0=src, scalar=w, in1=seed, op0=ALU.mult, op1=ALU.add)
                        else:
                            ins = nc.vector.tensor_scalar(a, src, w, None, ALU.mult)
                        ins.then_inc(mixed, 1)

                def hidden(it, k, first=False):
                    if not first or k:
                        dve.wait_ge(hsum_ready, count(it, k, 1, 0))
                    mixture(it, k, 0, bank[0:2], l1_done, acc1, mixed1)

                def output_mixture(it, k):
                    mixture(it, k, 1, bank[3:5], l2_done, acc2, mixed2, seed=row(x1_all, it, k))
                    dve.wait_ge(mixed2, count(it, k, DVE_E, 2 * DVE_E))
                    nc.vector.tensor_tensor(pair2[:], acc2[:, 0, :], acc2[:, 1, :], ALU.add).then_inc(pair2_ready, 1)

                def output_sum(it, k, fresh):
                    dve.wait_ge(pair2_ready, count(it, k, 1, 1))
                    dve.wait_ge(rest3_ready, count(it, k, 1, 2))
                    if fresh:
                        dve.wait_ge(oc_ready, it * BODY + BODY)
                    nc.vector.tensor_tensor(ysum[:, k, :], pair2[:], rest3[:], ALU.add).then_inc(ysum_ready, 1)
                    dve.wait_ge(ysum_ready, count(it, k, 1, 2))
                    nc.vector.bn_stats(ostats[:], ysum[:, k, :]).then_inc(ostep, 1)
                    dve.wait_ge(ostep, count(it, k, 1, 1))
                    dve.sem_inc(passed, 1)
                    nc.vector.bn_aggr(omv[:, k, :], ostats[:]).then_inc(ovar_ready, 1)

                def outputs(it):
                    dve.wait_ge(osd_ready, it + 1)
                    nc.vector.reciprocal(ors[:], osd[:]).then_inc(ors_ready, 1)
                    dve.wait_ge(ors_ready, it + 1)
                    for k in range(BODY):
                        dve.wait_ge(out_saved[k], (it + 1) * 16)
                        nc.vector.tensor_scalar(oc[k][:], ysum[:, k, :], omv[:, k, 0:1], ors[:, k:k + 1], ALU.subtract, ALU.mult)\
                          .then_inc(oc_ready, 1)

                def chunk(it, k, left):
                    output_mixture(it, k)
                    if k == BODY - 1:
                        output_sum(it, k, False)
                    if left >= 2:
                        hidden(it, k + 2)
                    if k < BODY - 1:
                        output_sum(it, k, False)
                    else:
                        outputs(it)

                hidden(0, 0, first=True)
                hidden(0, 1, first=True)
                with dve.Fori(0, NIT - 1) as it:
                    for k in range(BODY):
                        chunk(it, k, BODY)
                for k in range(BODY):
                    chunk(NIT - 1, k, BODY - 1 - k)


def kernel(**inputs):
    import concourse.bacc as bacc
    from concourse.bass_utils import run_bass_kernel_spmd

    a = {n.removeprefix("L0_"): np.asarray(v) for n, v in inputs.items()}
    x = np.ascontiguousarray(a["attn_hidden_states"].reshape(T, D))
    consts, sents = shape_constants()
    arrays = {
        "x": x,
        "xT": np.ascontiguousarray(x.T),
        "wqk": np.concatenate([a["attn_Wq"], a["attn_Wk"]], axis=1),
        "wkv": np.concatenate([a["attn_Wv"], a["attn_Wk"]], axis=1),
        "wo": np.ascontiguousarray(a["attn_Wo"]),
        "p_w": np.ascontiguousarray(a["ffn_P_w"]),
        "uT": np.ascontiguousarray(np.concatenate([a["ffn_U1"], a["ffn_U2"], a["ffn_U3"]], axis=0).T),
        "w1T": np.ascontiguousarray(a["ffn_W1"].transpose(2, 0, 1).reshape(D, NE * D)),
        "w2T": np.ascontiguousarray(a["ffn_W2"].transpose(2, 0, 1).reshape(D, NE * D)),
        "b2": np.ascontiguousarray(a["ffn_b2"]),
        "consts": consts,
        "sents": sents,
    }
    nc = bacc.Bacc("TRN2", target_bir_lowering=False, num_devices=1)
    handles = [nc.dram_tensor(n, list(v.shape), F32, kind="ExternalInput").ap() for n, v in arrays.items()]
    out = nc.dram_tensor("out", [T, D], F32, kind="ExternalOutput").ap()
    block_kernel(nc, *handles, out)
    r = run_bass_kernel_spmd(nc, [arrays], core_ids=[0])
    return r.results[0]["out"].reshape(1, T, D)
```

```python
from contextlib import ExitStack

import numpy as np
import concourse.bass as bass
from concourse import mybir

F32 = mybir.dt.float32
BF16 = mybir.dt.bfloat16
F32R = mybir.dt.float32r
ALU = mybir.AluOpType
ACT = mybir.ActivationFunctionType
AX_X = mybir.AxisListType.X

T, D = 2048, 128
NH, DK, DV = 16, 16, 64
P = 128
NCH = T // P
BODY = 4
NIT = NCH // BODY
PAIR = 2 * P
GRP = 512
NA = DK + 1
NF = NA * (NA + 1) // 2
NX = NF - P
KFW = P + 32
DE = DV + 1
VW = DE + 1
HALVES = (slice(0, P // 2), slice(P // 2, P))
HPG = 4
NG = NH // HPG
HPB = 7
EPS_Z, EPS_LN = 1e-12, 1e-5
NPIECE = 6
Q_PARTS = (0, 1, 0, 2, 0, 1)
K_PARTS = (0, 0, 1, 0, 2, 1)
KS = NPIECE * DK
NE, NR, TOPK = 12, 3, 3
EU = 4
NU = NE // EU
ZW = NE + 5
SENT = 3.0e38


def shape_constants():
    form = np.zeros((DK, NF), np.float32)
    bias = np.zeros(NF, np.float32)
    for d in range(NF // NA):
        for i in range(NA):
            for j in {i, (i + d) % NA}:
                if j < DK:
                    form[j, d * NA + i] = 0.25
                else:
                    bias[d * NA + i] = 1.0
    stacked = np.zeros((KS, NF), np.float32)
    for part in range(3):
        r = Q_PARTS.index(part) * DK
        stacked[r:r + DK] = form
    c = np.zeros((P, 2 * P + P + 32 + 4), np.float32)
    c[:, 0:P] = np.eye(P)
    c[:, P:2 * P] = np.triu(np.ones((P, P)))
    c[0:KS, 2 * P:2 * P + P] = stacked[:, 0:P]
    c[0:KS, 3 * P:3 * P + NX] = stacked[:, P:NF]
    c[:, 3 * P + 32] = bias[0:P]
    for j in range(HPG):
        c[32 * j:32 * j + NX, 3 * P + 33] = bias[P:NF]
    c[:, 3 * P + 34] = 1.0
    c[:, 3 * P + 35] = EPS_LN
    sentinels = np.tile(-SENT / 2.0 ** np.arange(5, dtype=np.float32), (P, NR, 1)).astype(np.float32)
    return c, sentinels


def count(it, k, per, extra):
    return it * (BODY * per) + (k * per + extra)


def row(tile, it, k):
    if isinstance(it, int):
        return tile[:, it * BODY + k]
    return tile[:, bass.ds(it * BODY + k, 1)].squeeze(1)


def columns(tile, it, k):
    if isinstance(it, int):
        return tile[:, (it * BODY + k) * P:(it * BODY + k + 1) * P]
    return tile[:, bass.ds(it * (BODY * P) + k * P, P)]


def block_kernel(nc, x, xT, wqk, wkv, wo, p_w, uT, w1T, w2T, b2, consts, sents, out):
    parts_dram = nc.dram_tensor("qk_parts", [3, 2, NH * DK, T], BF16, kind="Internal").ap()
    with ExitStack() as ctx:
        def sb(name, shape, dt=F32):
            return ctx.enter_context(nc.sbuf_tensor(name, shape, dt))

        def sem(name):
            return ctx.enter_context(nc.semaphore(name))

        bank = [ctx.enter_context(nc.psum_tensor(f"bank{b}", [P, 512], F32)) for b in range(8)]
        state_bank, prep_bank, out_bank = bank[0:3], bank[3:6], bank[6:8]

        x_all = sb("x_all", [P, NCH, D])
        xT_all = sb("xT_all", [D, T])
        wqk_sb = sb("wqk_sb", [D, 2 * NH * DK])
        w_raw = sb("w_raw", [D, NE * D])
        wkv_sb = w_raw[:, 0:NH * DV + NH * DK]
        wkv_hi, wkv_lo = (sb(f"wkv_{n}", [D, NH * DV + NH * DK], F32R) for n in ("hi", "lo"))
        wo_sb = sb("wo_sb", [P, NH * DV // P, D])
        cst = sb("cst", [P, 3 * P + 36])
        ident, mask = cst[:, 0:P], cst[:, P:2 * P]
        main_bias, rest_bias = cst[:, 3 * P + 32:3 * P + 33], cst[:, 3 * P + 33:3 * P + 34]
        one_col, eps_col = cst[:, 3 * P + 34:3 * P + 35], cst[:, 3 * P + 35:3 * P + 36]
        form_bf = sb("form_bf", [P, P + 32], BF16)
        zeros = sb("zeros", [P, 512], BF16)
        pw_sb = sb("pw_sb", [64, D])
        uT_sb = sb("uT_sb", [64, NR * NE])
        route_w = sb("route_w", [D, P])
        b2_sb = sb("b2_sb", [P, D])
        sent_sb = sb("sent_sb", [P, NR, 5])

        x1_all = sb("x1_all", [P, NCH, D])
        x1T_all = sb("x1T_all", [D, T])
        z_all = sb("z_all", [P, NCH, NR, NE])
        zm_all = sb("zm_all", [P, NCH, NR, NE])
        zmax_all = sb("zmax_all", [P, NCH, NR])
        ex = sb("ex", [P, NCH, NR, NE])
        wsum = sb("wsum", [P, NCH, NR])
        wr = sb("wr", [P, NCH, NR])
        mix_all = sb("mix_all", [P, NCH, NR, NE])
        cw = [sb(f"cw{b}", [P, P]) for b in range(BODY)]

        x_hi, x_lo = sb("x_hi", [D, P], F32R), sb("x_lo", [D, P], F32R)
        qf = sb("qf", [P, NH, P])
        qx = sb("qx", [P, NG, P])
        sq = sb("sq", [P, NH, P])
        at = sb("at", [P, NH, P])
        v1 = sb("v1", [P, NH, VW])
        k2 = sb("k2", [P, NH, 2 * NA])
        ksum = sb("ksum", [P, NH])
        kdiag = sb("kdiag", [P, NH, NA])
        kf = sb("kf", [P, NH, KFW])
        st = sb("st", [P, NH, VW])
        sx = sb("sx", [P, NG, HPG, DE])
        den = sb("den", [P, NH])
        rden = sb("rden", [P, NH])
        yn = sb("yn", [P, NH, DV])
        yT = sb("yT", [P, NH * DV // P, P])
        res = sb("res", [P, D])
        stats = sb("stats", [P, 6])
        mv = sb("mv", [P, 2])
        table_probe = sb("table_probe", [P, 1])
        sd = sb("sd", [P, 1])
        rs = sb("rs", [P, 1])
        x1c = sb("x1c", [P, D])
        x1T = sb("x1T", [D, P])
        zc = sb("zc", [P, NR, ZW])
        top = sb("top", [P, NR, 8])
        zm = sb("zm", [P, NR, ZW])

        with ExitStack() as room:
            def part_tile(name, dt=BF16):
                return room.enter_context(nc.sbuf_tensor(name, [P, 4, GRP], dt))

            hi = [part_tile(f"hi{b}") for b in range(2)]
            mid = [part_tile(f"mid{b}") for b in range(2)]
            low = [part_tile(f"low{b}") for b in range(2)]
            rem = part_tile("rem", F32)
        w1_hi, w1_lo, w2_hi, w2_lo = (sb(n, [D, NE * D], F32R) for n in ("w1_hi", "w1_lo", "w2_hi", "w2_lo"))
        xb = [sb(f"xb{b}", [D, P]) for b in range(BODY)]
        xb_hi, xb_lo = ([sb(f"xb_{n}{b}", [D, P], F32R) for b in range(2)] for n in ("hi", "lo"))
        acc1, acc2 = sb("acc1", [P, 2, D]), sb("acc2", [P, 2, D])
        ostats = sb("ostats", [P, 6])
        half1, half2 = sb("half1", [P, 2, D]), sb("half2", [P, 2, D])
        hsum = [sb(f"hsum{b}", [P, D]) for b in range(2)]
        pair1, pair2 = sb("pair1", [P, D]), sb("pair2", [P, D])

        with ExitStack() as room:
            q_st, k_st = ([room.enter_context(nc.sbuf_tensor(f"{n}_st{b}", [KS, NH, PAIR], BF16)) for b in range(2)]
                          for n in "qk")
        prod1, prod2 = sb("prod1", [P, EU, D]), sb("prod2", [P, EU, D])
        rest1, rest2 = sb("rest1", [P, D]), sb("rest2", [P, D])
        hh = [sb(f"hh{b}", [P, D]) for b in range(2)]
        c3b2 = sb("c3b2", [P, D])
        hT = sb("hT", [P, P])
        hT_hi, hT_lo = sb("hT_hi", [P, P], F32R), sb("hT_lo", [P, P], F32R)
        cT = sb("cT", [P, P])
        omv_c = sb("omv_c", [P, 2])
        omv, osd, ors = sb("omv", [P, NCH, 2]), sb("osd", [P, NCH]), sb("ors", [P, NCH])

        in_qk, in_xT, in_kv, in_cst, in_routers, in_x, in_wo, in_w1, in_w2, in_b2 = (
            sem(f"loaded_{n}") for n in ("wqk_and_first_x", "xT", "wkv", "consts", "routers", "x", "wo", "w1", "w2", "b2"))
        proj_done, hi_ready, rem_ready = sem("proj_done"), sem("hi_ready"), sem("rem_ready")
        mid_ready_a, mid_ready_v = sem("mid_ready_scalar"), sem("mid_ready_vector")
        low_ready, low_ready_g = sem("low_ready"), sem("low_ready_gpsimd")
        stored = [[sem(f"parts_stored{b}_{n}") for n in "qk"] for b in range(2)]
        stacked = [sem(f"stacked{b}") for b in range(2)]
        init_v, init_g = sem("init_vector"), sem("init_gpsimd")
        qf_done, qx_done, s_done, kv_done = sem("qf_done"), sem("qx_done"), sem("s_done"), sem("kv_done")
        y_done, st_done, yt_done, wo_done = sem("y_done"), sem("st_done"), sem("yt_done"), sem("wo_done")
        x1t_done, z_done, rw_done = sem("x1t_done"), sem("z_done"), sem("rw_done")
        qf_ready, qx_ready, sq_ready, v_ready = sem("qf_ready"), sem("qx_ready"), sem("sq_ready"), sem("v_ready")
        st_ready, yt_ready, sd_ready, x1t_ready = sem("st_ready"), sem("yt_ready"), sem("sd_ready"), sem("x1t_ready")
        at_ready, k2_ready, kd_ready, kp_ready = sem("at_ready"), sem("k2_ready"), sem("kd_ready"), sem("kp_ready")
        yn_ready, var_ready, x1_ready = sem("yn_ready"), sem("var_ready"), sem("x1_ready")
        z_ready, x_parts_ready, rw_ready = sem("z_ready"), sem("x_parts_ready"), sem("rw_ready")
        x1_saved, zsaved = sem("x1_saved"), sem("z_saved")
        dve_step = sem("dve_step")
        passed, passed_g = sem("passed"), sem("passed_gpsimd")

        x1t_saved, wkv_ready = sem("x1t_saved"), sem("wkv_parts_ready")
        N_INIT_V, N_INIT_G = 4, 7
        SPLIT = (slice(0, NCH - BODY), slice(NCH - BODY, NCH))
        STORED = 3 * 16

        mix_step, shift_ready, exp_ready, mix_ready = (sem(n) for n in ("mix_step", "shift_ready", "exp_ready", "mix_ready"))
        cw_ready, l1_done, l2_done, turned, took = (sem(n) for n in ("cw_ready", "l1_done", "l2_done", "turned", "took"))
        xb_loaded = [sem(f"xb_loaded{b}") for b in range(BODY)]
        b2_ready = sem("b2_ready")
        x1_hi_ready, x1_lo_ready = sem("x1T_hi_ready"), sem("x1T_lo_ready")
        w_hi_ready, w_lo_ready, h_lo_ready = sem("w_hi_ready"), sem("w_lo_ready"), sem("hidden_lo_ready")
        b2_done, mixed1, mixed2 = sem("b2_done"), sem("mixed1"), sem("mixed2")
        prod1_ready, prod2_ready = sem("prod1_ready"), sem("prod2_ready")
        hsum_ready, h_ready, half1_ready = (sem(n) for n in ("hsum_ready", "h_ready", "half1_ready"))
        sum_step, rest2_ready, pair2_ready = (sem(n) for n in ("sum_step", "rest2_ready", "pair2_ready"))
        ysum_ready, ovar_ready, ostep = sem("ysum_ready"), sem("ovar_ready"), sem("ostep")
        osd_ready, ors_ready, oc_ready = sem("osd_ready"), sem("ors_ready"), sem("oc_ready")
        out_saved = sem("out_saved")
        DVE_E = 2 * EU

        with nc.Block() as block:
            @block.sync
            def _(sp):
                sp.dma_start(wqk_sb[:], wqk).then_inc(in_qk, 16)
                sp.dma_start(xT_all[:, 0:GRP], xT[:, 0:GRP]).then_inc(in_qk, 16)
                sp.dma_start(xT_all[:, GRP:T], xT[:, GRP:T]).then_inc(in_xT, 16)
                sp.dma_start(cst[:], consts).then_inc(in_cst, 16)
                sp.dma_start(wkv_sb, wkv).then_inc(in_kv, 16)
                sp.dma_start(pw_sb[:], p_w).then_inc(in_routers, 16)
                sp.dma_start(uT_sb[:], uT).then_inc(in_routers, 16)
                sp.dma_start(sent_sb[:], sents).then_inc(in_routers, 16)

                def store_parts(g):
                    for which in range(2):
                        sp.wait_ge(low_ready, g + 2)
                        sp.wait_ge(low_ready_g, 3 * g + (4, 6)[which])
                        for part, tile in enumerate((hi, mid, low)):
                            dst = parts_dram[part, which, :, g * GRP:(g + 1) * GRP].rearrange("(t p) n -> p t n", p=P)
                            sp.dma_start(dst, tile[g % 2][:, 2 * which:2 * which + 2, :]).then_inc(stored[g % 2][which], 16)

                def load_pair(b, p):
                    for which, (dst, parts) in enumerate(((q_st[b], Q_PARTS), (k_st[b], K_PARTS))):
                        for j, part in enumerate(parts):
                            src = parts_dram[part, which, :, bass.ds(p * PAIR, PAIR)]
                            sp.dma_start(dst[j * DK:(j + 1) * DK, :, :],
                                         src.rearrange("(h i) n -> i h n", i=DK)).then_inc(stacked[b], 16)

                store_parts(0)
                store_parts(1)
                for which in range(2):
                    sp.wait_ge(stored[0][which], STORED * 2)
                load_pair(0, 0)
                load_pair(1, 1)
                store_parts(2)
                store_parts(3)
                sp.dma_start(x_all[:], x.rearrange("(c p) d -> p c d", p=P)).then_inc(in_x, 16)
                sp.dma_start(wo_sb[:], wo.rearrange("(t p) d -> p t d", p=P)).then_inc(in_wo, 16)
                for b in range(2):
                    for which in range(2):
                        sp.wait_ge(stored[b][which], STORED * 3)
                sp.wait_ge(wkv_ready, 2)
                sp.dma_start(w_raw[:], w1T).then_inc(in_w1, 16)
                with sp.Fori(0, NIT - 1) as it:
                    for b in range(2):
                        sp.wait_ge(s_done, count(it, 2 * b + 2, NG, 0))
                        load_pair(b, it * 2 + (2 + b))

                def stage(it, k):
                    sp.dma_start(xb[k % BODY][:], columns(x1T_all, it, k)).then_inc(xb_loaded[k % BODY], 16)

                sp.wait_ge(w_lo_ready, 1)
                sp.dma_start(w_raw[:], w2T).then_inc(in_w2, 16)
                sp.wait_ge(x1t_saved, BODY + 1)
                for k in range(BODY):
                    stage(0, k)
                sp.wait_ge(x1t_saved, NCH + 1)
                with sp.Fori(0, NIT - 1) as it:
                    for k in range(BODY):
                        sp.wait_ge(x1_lo_ready, count(it, k, 1, 1))
                        stage(it, k + BODY)
                for g in range(NIT):
                    sp.wait_ge(oc_ready, BODY * (g + 1))
                    sp.dma_start(out[g * BODY * P:(g + 1) * BODY * P, :].rearrange("(c p) d -> p c d", p=P),
                                 x1_all[:, g * BODY:(g + 1) * BODY, :]).then_inc(out_saved, 16)
                sp.wait_ge(out_saved, 16 * NIT)

            @block.tensor
            def _(pe):
                pe.wait_ge(in_qk, 32)
                with pe.Fori(0, T // GRP // 2) as gg:
                    for b in range(2):
                        if b == 1:
                            pe.wait_ge(in_xT, 16)
                        for t in range(4):
                            pe.wait_ge(rem_ready, gg * 8 + (4 * b + t + 1))
                            nc.tensor.matmul(bank[4 * b + t][:], wqk_sb[:, t * P:(t + 1) * P],
                                             xT_all[:, bass.ds(gg * (2 * GRP) + b * GRP, GRP)],
                                             start=True, stop=True).then_inc(proj_done, 1)
                pe.wait_ge(init_g, N_INIT_G)
                pe.wait_ge(rem_ready, 4 * (T // GRP) + 4)
                for b in range(3):
                    nc.tensor.matmul(state_bank[b][:], zeros[:, 0:P], zeros[:], start=True, stop=True)
                pe.wait_ge(rem_ready, 4 * (T // GRP) + 6)
                pe.wait_ge(init_v, 1)

                def query_features(it, k, g):
                    b, off = (k // 2) % 2, (k % 2) * P
                    nc.tensor.matmul(prep_bank[g % 3][:], form_bf[0:KS, 0:P],
                                     q_st[b][:, HPG * g:HPG * g + HPG, off:off + P],
                                     start=True, stop=True).then_inc(qf_done, 1)

                def query_rest(it, k):
                    b, off = (k // 2) % 2, (k % 2) * P
                    for j in range(HPG):
                        mm = nc.tensor.matmul(prep_bank[1][32 * j:32 * j + 32, :], form_bf[0:KS, P:P + 32],
                                              q_st[b][:, j:NH:HPG, off:off + P], start=True, stop=True)
                    mm.then_inc(qx_done, 1)

                def scores(it, k, g):
                    b, off = (k // 2) % 2, (k % 2) * P
                    for j in range(HPG):
                        h = HPG * g + j
                        mm = nc.tensor.matmul(prep_bank[(5 + g) % 3][:, j * P:(j + 1) * P],
                                              k_st[b][:, h, off:off + P], q_st[b][:, h, off:off + P],
                                              start=True, stop=True)
                    mm.then_inc(s_done, 1)

                def keys_values(it, k, u):
                    n = 512 if u < 2 else NH * DK
                    for i, (xp, wp) in enumerate(((x_hi, wkv_hi), (x_hi, wkv_lo), (x_lo, wkv_hi))):
                        mm = nc.tensor.matmul(prep_bank[u][:, 0:n], xp[:], wp[:, u * 512:u * 512 + n],
                                              start=(i == 0), stop=(i == 2))
                    mm.then_inc(kv_done, 1)

                def prep_group(it, k, g):
                    if g == 0:
                        pe.wait_ge(v_ready, count(it, k, 2, 1))
                        if k % 2 == 0:
                            pe.wait_ge(stacked[(k // 2) % 2], (it + (k // BODY + 1)) * (2 * NPIECE * 16))
                    if g == 1:
                        pe.wait_ge(v_ready, count(it, k, 2, 2))
                    if g == 2:
                        pe.wait_ge(k2_ready, count(it, k, 1, 1))
                    if g == 3:
                        pe.wait_ge(qf_ready, count(it, k, NG, 1))
                    query_features(it, k, g)

                def prep_rest(it, k):
                    pe.wait_ge(qf_ready, count(it, k, NG, 2))
                    query_rest(it, k)

                def prep_scores(it, k, g):
                    if g < 2:
                        pe.wait_ge(qf_ready, count(it, k, NG, 3 + g))
                    elif g == 2:
                        pe.wait_ge(qx_ready, count(it, k, 1, 1))
                    else:
                        pe.wait_ge(sq_ready, count(it, k, NG, 1))
                    scores(it, k, g)

                def prep_kv(it, k, u):
                    pe.wait_ge(sq_ready, count(it, k, NG, 2 + u))
                    if u == 0:
                        pe.wait_ge(x_parts_ready, count(it, k, 2, 2))
                    keys_values(it, k, u)

                def attend(it, k, g):
                    ob = out_bank[(9 * k + g) % 2]
                    if g + k == 0:
                        pe.wait_ge(rw_ready, 1)
                    if g == 0:
                        pe.wait_ge(x1t_ready, count(it, k, 1, 1))
                        pe.wait_ge(st_ready, count(it, k, 1, 1))
                        pe.wait_ge(qx_ready, count(it, k, 1, 1))
                    elif g == 1:
                        pe.wait_ge(z_ready, count(it, k, 1, 1))
                    else:
                        pe.wait_ge(yn_ready, count(it, k, NG, g - 1))
                    pe.wait_ge(qf_ready, count(it, k, NG, g + 1))
                    pe.wait_ge(at_ready, count(it, k, NG, g + 1))
                    nc.tensor.matmul(ob[:, 0:HPG * DE], qx[:, g, :], sx[:, g, :, :].rearrange("p a b -> p (a b)"),
                                     start=True, stop=False, skip_group_check=True)
                    for j in range(HPG):
                        h = HPG * g + j
                        for half in HALVES:
                            nc.tensor.matmul(ob[half, j * DE:j * DE + VW], qf[:, h, half], st[:, h, :],
                                             start=False, stop=False, skip_group_check=True)
                        if h % 8 == 0:
                            pe.wait_ge(v_ready, count(it, k, 2, 3 + h // 8))
                        for half in HALVES:
                            mm = nc.tensor.matmul(ob[half, j * DE:j * DE + VW], at[:, h, half], v1[:, h, :],
                                                  start=False, stop=(j == HPG - 1), skip_group_check=True)
                    mm.then_inc(y_done, 1)

                def grow_state(it, k, b):
                    if b == 0:
                        pe.wait_ge(kd_ready, count(it, k, 1, 1))
                        pe.wait_ge(kp_ready, count(it, k, 1, 2))
                    for h in range(HPB * b, min(HPB * (b + 1), NH)):
                        for half in HALVES:
                            o = state_bank[b][half, (h - HPB * b) * DE:(h - HPB * b) * DE + VW]
                            mm = nc.tensor.matmul(o, kf[:, h, half], v1[:, h, :], start=False, stop=True,
                                                  skip_group_check=True)
                    if b < 2:
                        mm.then_inc(st_done, 1)

                def grow_rest(it, k):
                    for h in range(NH):
                        g, j = h // HPG, h % HPG
                        o = state_bank[2][32 * j:32 * j + 32, (2 + g) * DE:(2 + g) * DE + VW]
                        mm = nc.tensor.matmul(o, kf[:, h, P:KFW], v1[:, h, :], start=False, stop=True,
                                              skip_group_check=True)
                    mm.then_inc(st_done, 1)

                def turn_y(it, k, u):
                    ob = out_bank[(9 * k + 4 + u) % 2]
                    pe.wait_ge(yn_ready, count(it, k, NG, 4 if u else 3))
                    for j in range(4):
                        y2 = yn[:].rearrange("p h e -> p (h e)")
                        mm = nc.tensor.transpose(ob[:, j * P:(j + 1) * P], y2[:, (4 * u + j) * P:(4 * u + j + 1) * P], ident)
                    mm.then_inc(yt_done, 1)

                def project_y(it, k):
                    ob = out_bank[(9 * k + 6) % 2]
                    if k == 0:
                        pe.wait_ge(in_wo, 16)
                    pe.wait_ge(yt_ready, count(it, k, 2, 2))
                    for j in range(NH * DV // P):
                        mm = nc.tensor.matmul(ob[:, 0:D], yT[:, j, :], wo_sb[:, j, :],
                                              start=(j == 0), stop=(j == NH * DV // P - 1))
                    mm.then_inc(wo_done, 1)

                def turn_x1(it, k):
                    ob = out_bank[(9 * k + 7) % 2]
                    pe.wait_ge(x1_ready, count(it, k, 1, 1))
                    nc.tensor.transpose(ob[:, 0:P], x1c[:], ident).then_inc(x1t_done, 1)

                def route(it, k):
                    ob = out_bank[(9 * k + 8) % 2]
                    pe.wait_ge(x1t_ready, count(it, k, 1, 2))
                    nc.tensor.matmul(ob[:, 0:P], x1T[:], route_w[:], start=True, stop=True).then_inc(z_done, 1)

                def chunk(it, k):
                    n = k + 1
                    for g in range(NG):
                        attend(it, k, g)
                        prep_group(it, n, g)
                    grow_state(it, k, 0)
                    prep_rest(it, n)
                    prep_scores(it, n, 0)
                    prep_scores(it, n, 1)
                    turn_y(it, k, 0)
                    turn_y(it, k, 1)
                    grow_state(it, k, 1)
                    grow_state(it, k, 2)
                    prep_scores(it, n, 2)
                    project_y(it, k)
                    prep_scores(it, n, 3)
                    grow_rest(it, k)
                    prep_kv(it, n, 0)
                    prep_kv(it, n, 2)
                    turn_x1(it, k)
                    prep_kv(it, n, 1)
                    route(it, k)

                for g in range(NG):
                    prep_group(0, 0, g)
                prep_rest(0, 0)
                for g in range(NG):
                    prep_scores(0, 0, g)
                pe.wait_ge(wkv_ready, 2)
                for u in (0, 2, 1):
                    prep_kv(0, 0, u)
                pe.wait_ge(rem_ready, 4 * (T // GRP) + 8)
                pe.wait_ge(in_routers, 16 * 3)
                nc.tensor.matmul(out_bank[0][:, 0:NR * NE], pw_sb[:], uT_sb[:], start=True, stop=True).then_inc(rw_done, 1)
                with pe.Fori(0, NIT - 1) as it:
                    for k in range(BODY):
                        chunk(it, k)
                for k in range(BODY - 1):
                    chunk(NIT - 1, k)

                def in_parts(dst, hi, lo, w_hi, w_lo, u):
                    cols = slice(u * EU * D, (u + 1) * EU * D)
                    nc.tensor.matmul(dst[:], hi[:], w_hi[:, cols], start=True, stop=False)
                    nc.tensor.matmul(dst[:], hi[:], w_lo[:, cols], start=False, stop=False)
                    return nc.tensor.matmul(dst[:], lo[:], w_hi[:, cols], start=False, stop=True)

                def first(it, k, units):
                    pe.wait_ge(x1_hi_ready, count(it, k, 1, 1))
                    pe.wait_ge(x1_lo_ready, count(it, k, 1, 1))
                    for u in units:
                        if u == 2:
                            pe.wait_ge(prod1_ready, count(it, k, 1, 1))
                        else:
                            pe.wait_ge(mixed1, count(it, k, DVE_E, EU * (u + 1)))
                        in_parts(bank[u], xb_hi[k % 2], xb_lo[k % 2], w1_hi, w1_lo, u).then_inc(l1_done, 1)

                def turn(it, k):
                    pe.wait_ge(took, count(it, k, 3, 3))
                    pe.wait_ge(h_ready, count(it, k, 1, 1))
                    pe.wait_ge(cw_ready, count(it, k, 1, 1))
                    nc.tensor.transpose(bank[6][:, 0:P], hh[k % 2][:], ident)
                    nc.tensor.transpose(bank[6][:, P:2 * P], cw[k % BODY][:], ident).then_inc(turned, 1)

                def second(it, k):
                    pe.wait_ge(took, count(it, k, 3, 6))
                    pe.wait_ge(h_lo_ready, count(it, k, 1, 1))
                    pe.wait_ge(mixed2, count(it, k, DVE_E, 2))
                    pe.wait_ge(prod2_ready, count(it, k, 1, 1))
                    nc.tensor.matmul(bank[7][:, 0:D], cT[:], b2_sb[:], start=True, stop=True).then_inc(b2_done, 1)
                    for u in (2, 0, 1):
                        if u < 2:
                            pe.wait_ge(mixed2, count(it, k, DVE_E, EU * (u + 1)))
                        in_parts(bank[3 + u], hT_hi, hT_lo, w2_hi, w2_lo, u).then_inc(l2_done, 1)

                def step_behind(it, k, left):
                    if left >= 2:
                        first(it, k + 2, (2, 0))
                    if left >= 1:
                        turn(it, k + 1)
                    if left >= 2:
                        first(it, k + 2, (1,))
                    if left >= 1:
                        second(it, k + 1)

                last = (NIT - 1, BODY - 1)
                for g in range(NG):
                    attend(*last, g)
                turn_y(*last, 0)
                turn_y(*last, 1)
                project_y(*last)
                pe.wait_ge(w_hi_ready, 2)
                pe.wait_ge(w_lo_ready, 2)
                first(0, 0, (2, 0, 1))
                turn_x1(*last)
                first(0, 1, (2, 0))
                route(*last)
                first(0, 1, (1,))
                pe.wait_ge(in_b2, 16)
                pe.wait_ge(z_ready, NCH + 1)
                turn(0, 0)
                second(0, 0)
                with pe.Fori(0, NIT - 1) as it:
                    for k in range(BODY):
                        step_behind(it, k, BODY)
                for k in range(BODY):
                    step_behind(NIT - 1, k, BODY - 1 - k)

            @block.scalar
            def _(act):
                def part(t, dst, src, ready):
                    nc.scalar.activation(dst[:, t, :], src, ACT.Copy).then_inc(ready, 1)

                act.sem_inc(st_ready, 1)
                act.sem_inc(v_ready, 2)
                act.sem_inc(x1t_ready, 1)
                for b in range(2):
                    for which in range(2):
                        act.sem_inc(stored[b][which], STORED)

                def high(g, t):
                    act.wait_ge(proj_done, 4 * g + t + 1)
                    act.wait_ge(stored[g % 2][t // 2], (g // 2 + 1) * STORED)
                    part(t, hi[g % 2], bank[4 * (g % 2) + t][:], hi_ready)

                def middle(g, t):
                    act.wait_ge(rem_ready, 8 + 4 * g + t + 1)
                    part(t, mid[g % 2], rem[:, t, :], mid_ready_a)

                for g in range(T // GRP):
                    high(g, 0)
                    if g:
                        middle(g - 1, 3)
                    high(g, 1)
                    high(g, 2)
                    middle(g, 1)
                    high(g, 3)
                middle(T // GRP - 1, 3)
                act.wait_ge(in_cst, 16)

                def load_table(function):
                    nc.scalar.activation(table_probe[:], one_col, function)

                def query_squares(it, k, g):
                    act.wait_ge(qf_done, count(it, k, NG, g + 1))
                    nc.scalar.activation(qf[:, HPG * g:HPG * g + HPG, :],
                                         prep_bank[g % 3][:].rearrange("p (h n) -> p h n", h=HPG),
                                         ACT.Square, bias=main_bias).then_inc(qf_ready, 1)

                def rest_squares(it, k):
                    act.wait_ge(qx_done, count(it, k, 1, 1))
                    nc.scalar.activation(qx[:], prep_bank[1][:].rearrange("p (g n) -> p g n", g=NG),
                                         ACT.Square, bias=rest_bias).then_inc(qx_ready, 1)

                def score_squares(it, k, g, first=False):
                    act.wait_ge(s_done, count(it, k, NG, g + 1))
                    if not first:
                        act.wait_ge(at_ready, count(it, k, NG, g - 3))
                    nc.scalar.activation(sq[:, HPG * g:HPG * g + HPG, :],
                                         prep_bank[(5 + g) % 3][:].rearrange("p (h n) -> p h n", h=HPG),
                                         ACT.Square, bias=one_col, scale=0.25).then_inc(sq_ready, 1)

                def take_values(it, k, u):
                    act.wait_ge(kv_done, count(it, k, 3, 2 * u + 1))
                    nc.scalar.activation(v1[:, 8 * u:8 * u + 8, 0:DV], prep_bank[u][:].rearrange("p (h e) -> p h e", e=DV),
                                         ACT.Copy).then_inc(v_ready, 1)

                def take_state(it, k, b):
                    act.wait_ge(st_done, count(it, k, 3, b + 1))
                    n = min(HPB, NH - HPB * b)
                    nc.scalar.activation(st[:, HPB * b:HPB * b + n, 0:DE],
                                         state_bank[b][:, 0:n * DE].rearrange("p (h e) -> p h e", e=DE), ACT.Copy)
                    if b == 2:
                        for j in range(HPG):
                            rows = slice(32 * j, 32 * j + 32)
                            last = nc.scalar.activation(sx[rows, :, j, :],
                                                        state_bank[2][rows, 2 * DE:(2 + NG) * DE].rearrange("p (g e) -> p g e", e=DE),
                                                        ACT.Copy)
                        last.then_inc(st_ready, 1)

                def take_turned_y(it, k, u):
                    act.wait_ge(yt_done, count(it, k, 2, u + 1))
                    nc.scalar.activation(yT[:, 4 * u:4 * u + 4, :],
                                         out_bank[(9 * k + 4 + u) % 2][:].rearrange("p (j n) -> p j n", j=4),
                                         ACT.Copy).then_inc(yt_ready, 1)

                def deviation(it, k):
                    act.wait_ge(var_ready, count(it, k, 1, 1))
                    nc.scalar.activation(sd[:], mv[:, 1:2], ACT.Sqrt, bias=eps_col).then_inc(sd_ready, 1)

                def take_turned_x1(it, k):
                    act.wait_ge(x1t_done, count(it, k, 1, 1))
                    act.wait_ge(x1t_saved, count(it, k, 1, 1))
                    nc.scalar.activation(x1T[:], out_bank[(9 * k + 7) % 2][:, 0:P], ACT.Copy).then_inc(x1t_ready, 1)

                def routing_exp(half):
                    act.wait_ge(shift_ready, half + 1)
                    e = ex[:, SPLIT[half]].rearrange("p c r e -> p (c r e)")
                    nc.scalar.activation(e, e, ACT.Exp).then_inc(exp_ready, 1)

                def expert_weights_high(dst, loaded, piece):
                    if piece == 0:
                        act.wait_ge(loaded, 16)
                    cols = slice(piece * EU * D, (piece + 1) * EU * D)
                    cast = nc.scalar.activation(dst[:, cols], w_raw[:, cols], ACT.Copy)
                    if piece == NU - 1:
                        cast.then_inc(w_hi_ready, 1)

                def chunk(it, k, routing=False, weights=None):
                    n = k + 1
                    query_squares(it, n, 0)
                    if routing:
                        routing_exp(0)
                    for g in range(1, NG):
                        if weights:
                            expert_weights_high(*weights, g - 1)
                        query_squares(it, n, g)
                    take_state(it, k, 0)
                    rest_squares(it, n)
                    score_squares(it, n, 0)
                    take_turned_y(it, k, 0)
                    take_turned_y(it, k, 1)
                    score_squares(it, n, 1)
                    take_state(it, k, 1)
                    score_squares(it, n, 2)
                    score_squares(it, n, 3)
                    deviation(it, k)
                    take_state(it, k, 2)
                    take_turned_x1(it, k)
                    take_values(it, n, 0)
                    take_values(it, n, 1)

                for g in range(NG):
                    query_squares(0, 0, g)
                rest_squares(0, 0)
                for g in range(NG):
                    score_squares(0, 0, g, first=True)
                take_values(0, 0, 0)
                take_values(0, 0, 1)
                with act.Fori(0, NIT - 1) as it:
                    load_table(ACT.Sqrt)
                    for k in range(BODY):
                        chunk(it, k)
                load_table(ACT.Sqrt)
                for k in range(BODY - 1):
                    chunk(NIT - 1, k, routing=(k == 1), weights=((w1_hi, in_w1), None, (w2_hi, in_w2))[k])

                act.sem_inc(took, 3)
                act.sem_inc(prod1_ready, 1)
                act.sem_inc(prod2_ready, 1)

                def weigh(it, k, r, b, dst):
                    for j in range(EU):
                        e = (r * NE) + 2 * EU + j
                        last = nc.scalar.activation(dst[:, j, :], bank[b][:, j * D:(j + 1) * D], ACT.Copy,
                                                    scale=cw[k % BODY][:, e:e + 1])
                    return last

                def hidden_products(it, k):
                    act.wait_ge(cw_ready, count(it, k, 1, 1))
                    act.wait_ge(l1_done, count(it, k, NU, 1))
                    act.wait_ge(half1_ready, count(it, k, 1, 1))
                    weigh(it, k, 0, 2, prod1).then_inc(prod1_ready, 1)

                def output_products(it, k):
                    act.wait_ge(b2_done, count(it, k, 1, 1))
                    nc.scalar.activation(c3b2[:], bank[7][:, 0:D], ACT.Copy).then_inc(b2_ready, 1)
                    act.wait_ge(l2_done, count(it, k, NU, 1))
                    act.wait_ge(rest2_ready, count(it, k, 1, 1))
                    weigh(it, k, 1, 5, prod2).then_inc(prod2_ready, 1)

                def gelu(it, k):
                    act.wait_ge(hsum_ready, count(it, k, 1, 1))
                    nc.scalar.activation(hh[k % 2][:], hsum[k % 2][:], ACT.Gelu).then_inc(h_ready, 1)

                def take(it, k):
                    act.wait_ge(turned, count(it, k, 1, 1))
                    nc.scalar.activation(hT_hi[:], bank[6][:, 0:P], ACT.Copy).then_inc(took, 1)
                    nc.scalar.activation(hT[:], bank[6][:, 0:P], ACT.Copy).then_inc(took, 1)
                    nc.scalar.activation(cT[:], bank[6][:, P:2 * P], ACT.Copy).then_inc(took, 1)

                def deviations(half):
                    c = SPLIT[half]
                    act.wait_ge(ovar_ready, c.stop)
                    nc.scalar.activation(osd[:, c], omv[:, c, 1], ACT.Sqrt, bias=eps_col).then_inc(osd_ready, 1)

                def x1_high(it, k, earlier=True):
                    act.wait_ge(xb_loaded[k % BODY], (it + (k // BODY + 1)) * 16)
                    if earlier:
                        act.wait_ge(l1_done, count(it, k, NU, -NU))
                    nc.scalar.activation(xb_hi[k % 2][:], xb[k % BODY][:], ACT.Copy).then_inc(x1_hi_ready, 1)

                def expert_chunk(it, k, left):
                    output_products(it, k)
                    if left >= 1:
                        gelu(it, k + 1)
                        take(it, k + 1)
                    if left >= 2:
                        hidden_products(it, k + 2)
                    if left >= 3:
                        x1_high(it, k + 3)

                x1_high(0, 0, earlier=False)
                x1_high(0, 1, earlier=False)
                last = (NIT - 1, BODY - 1)
                take_turned_y(*last, 0)
                take_turned_y(*last, 1)
                deviation(*last)
                hidden_products(0, 0)
                take_turned_x1(*last)
                hidden_products(0, 1)
                x1_high(0, 2)
                gelu(0, 0)
                take(0, 0)
                routing_exp(1)
                with act.Fori(0, NIT - 1) as it:
                    load_table(ACT.Gelu)
                    for k in range(BODY):
                        expert_chunk(it, k, BODY)
                for k in range(BODY):
                    expert_chunk(NIT - 1, k, BODY - 1 - k)
                    if k == 1:
                        deviations(0)
                deviations(1)

            @block.vector
            def _(dve):
                dve.sem_inc(rem_ready, 8)
                dve.sem_inc(low_ready, 1)
                dve.sem_inc(k2_ready, 1)
                dve.sem_inc(z_ready, 1)
                dve.wait_ge(in_cst, 16)
                nc.vector.tensor_copy(form_bf[:], cst[:, 2 * P:3 * P + 32]).then_inc(init_v, 1)
                nc.vector.memset(route_w[:], 0.0).then_inc(init_v, 1)
                nc.vector.memset(k2[:, :, DK:2 * NA:NA], 1.0).then_inc(init_v, 1)
                with dve.Fori(0, T // GRP // 2) as gg:
                    def remainder(b, t):
                        dve.wait_ge(hi_ready, gg * 8 + (4 * b + t + 1))
                        if t == 0:
                            dve.wait_ge(low_ready, gg * 2 + (b + 1))
                        else:
                            dve.wait_ge(low_ready_g, gg * 6 + (3 * b + t))
                        nc.vector.tensor_tensor(rem[:, t, :], bank[4 * b + t][:], hi[b][:, t, :], ALU.subtract).then_inc(rem_ready, 1)

                    def middle(b, t):
                        dve.wait_ge(rem_ready, gg * 8 + (4 * b + t + 9))
                        nc.vector.tensor_copy(mid[b][:, t, :], rem[:, t, :]).then_inc(mid_ready_v, 1)

                    def lowest(b, t):
                        dve.wait_ge(mid_ready_v, gg * 4 + (2 * b + t // 2 + 1))
                        nc.vector.tensor_tensor(low[b][:, t, :], rem[:, t, :], mid[b][:, t, :], ALU.subtract).then_inc(low_ready, 1)

                    for b in range(2):
                        remainder(b, 0)
                        remainder(b, 1)
                        middle(b, 0)
                        remainder(b, 2)
                        lowest(b, 0)
                        middle(b, 2)
                        remainder(b, 3)
                dve.wait_ge(in_kv, 16)
                nc.vector.tensor_copy(wkv_hi[:], wkv_sb).then_inc(wkv_ready, 1)
                dve.wait_ge(wkv_ready, 1)
                nc.vector.tensor_tensor(wkv_lo[:], wkv_sb, wkv_hi[:], ALU.subtract).then_inc(wkv_ready, 1)
                PER = 17
                at_chunk = [0, 0, 0]

                def step(ins):
                    it, k, done = at_chunk
                    ins.then_inc(dve_step, 1)
                    at_chunk[2] = done + 1
                    dve.wait_ge(dve_step, count(it, k, PER, done + 1))

                def normalize(it, k, g):
                    ob = out_bank[(9 * k + g) % 2][:, 0:HPG * DE].rearrange("p (h e) -> p h e", e=DE)
                    heads = slice(HPG * g, HPG * g + HPG)
                    dve.wait_ge(y_done, count(it, k, NG, g + 1))
                    step(nc.vector.tensor_scalar(den[:, heads], ob[:, :, DV], 2 * EPS_Z, None, ALU.add))
                    step(nc.vector.reciprocal(rden[:, heads], den[:, heads]))
                    nc.vector.tensor_tensor(yn[:, heads, :], ob[:, :, 0:DV],
                                            rden[:, heads].unsqueeze(2).broadcast_to([P, HPG, DV]),
                                            ALU.mult).then_inc(yn_ready, 1)

                def mask_scores(it, k, g):
                    heads = slice(HPG * g, HPG * g + HPG)
                    dve.wait_ge(sq_ready, count(it, k, NG, g + 1))
                    nc.vector.scalar_tensor_tensor(out=at[:, heads, :], in0=sq[:, heads, :], scalar=1.0,
                                                   in1=mask.unsqueeze(1).broadcast_to([P, HPG, P]),
                                                   op0=ALU.add, op1=ALU.mult).then_inc(at_ready, 1)

                def take_keys(it, k):
                    kb = prep_bank[2][:, 0:NH * DK].rearrange("p (h i) -> p h i", i=DK)
                    dve.wait_ge(kv_done, count(it, k, 3, 2))
                    dve.wait_ge(kp_ready, count(it, k, 1, 1))
                    nc.vector.tensor_copy(k2[:, :, 0:DK], kb)
                    nc.vector.tensor_copy(k2[:, :, NA:NA + DK], kb).then_inc(k2_ready, 1)

                def key_diagonal(it, k):
                    dve.wait_ge(k2_ready, count(it, k, 1, 2))
                    if k == 0:
                        dve.wait_ge(init_g, N_INIT_G)
                    step(nc.vector.reduce_sum(ksum[:], k2[:, :, 0:NA], AX_X))
                    step(nc.vector.scalar_tensor_tensor(out=kdiag[:], in0=k2[:, :, 0:NA], scalar=2.0,
                                                               in1=ksum[:].unsqueeze(2).broadcast_to([P, NH, NA]),
                                                               op0=ALU.mult, op1=ALU.subtract))
                    step(nc.vector.tensor_tensor(kf[:, :, 0:NA], kdiag[:], k2[:, :, 0:NA], ALU.mult))
                    nc.vector.tensor_scalar(kf[:, :, DK], kf[:, :, DK], 1.0, None, ALU.add).then_inc(kd_ready, 1)

                def add_residual(it, k):
                    if k == 0:
                        dve.wait_ge(in_x, 16)
                    dve.wait_ge(wo_done, count(it, k, 1, 1))
                    step(nc.vector.tensor_tensor(res[:], out_bank[(9 * k + 6) % 2][:, 0:D],
                                                        row(x_all, it, k), ALU.add))
                    step(nc.vector.bn_stats(stats[:], res[:]))
                    dve.sem_inc(passed, 1)
                    nc.vector.bn_aggr(mv[:], stats[:]).then_inc(var_ready, 1)

                def norm(it, k):
                    dve.wait_ge(sd_ready, count(it, k, 1, 1))
                    step(nc.vector.reciprocal(rs[:], sd[:]))
                    dve.wait_ge(x1_saved, count(it, k, 1, 1))
                    nc.vector.tensor_scalar(x1c[:], res[:], mv[:, 0:1], rs[:], ALU.subtract, ALU.mult).then_inc(x1_ready, 1)

                def take_routes(it, k):
                    dve.wait_ge(z_done, count(it, k, 1, 1))
                    nc.vector.tensor_copy(zc[:, :, 0:NE], out_bank[(9 * k + 8) % 2][:, 0:NR * NE].rearrange("p (r e) -> p r e", e=NE))\
                      .then_inc(z_ready, 1)

                def choose(it, k):
                    dve.wait_ge(z_ready, count(it, k, 1, 2))
                    dve.sem_inc(passed, 1)
                    for r in range(NR):
                        mx = nc.vector.max(out=top[:, r, :], in_=zc[:, r, 0:NE])
                    step(mx)
                    nc.vector.tensor_copy(row(zmax_all, it, k), top[:, :, 0])
                    step(nc.vector.tensor_copy(top[:, :, TOPK:8], sent_sb[:]))
                    dve.sem_inc(passed, 1)
                    for r in range(NR):
                        mr = nc.vector.match_replace(out=zm[:, r, :], in_to_replace=top[:, r, :], in_values=zc[:, r, :], imm_value=SENT)
                    step(mr)
                    nc.vector.tensor_copy(row(z_all, it, k), zc[:, :, 0:NE])
                    nc.vector.tensor_copy(row(zm_all, it, k), zm[:, :, 0:NE]).then_inc(zsaved, 1)

                def link(ins):
                    done[0] += 1
                    ins.then_inc(mix_step, 1)
                    dve.wait_ge(mix_step, done[0])

                done = [0]

                def routing_shift(half):
                    dve.wait_ge(zsaved, (NCH - BODY, NCH)[half])
                    c = ex[:, SPLIT[half]]
                    nc.vector.tensor_tensor(c.rearrange("p c r e -> p (c r) e"), z_all[:, SPLIT[half]].rearrange("p c r e -> p (c r) e"),
                                            zmax_all[:, SPLIT[half]].rearrange("p c r -> p (c r)").unsqueeze(2)
                                            .broadcast_to([P, c.shape[1] * NR, NE]), ALU.subtract).then_inc(shift_ready, 1)

                def routing_weights(half):
                    e, marked, mix = (t[:, SPLIT[half]].rearrange("p c r e -> p (c r) e") for t in (ex, zm_all, mix_all))
                    total, inverse = (t[:, SPLIT[half]].rearrange("p c r -> p (c r)") for t in (wsum, wr))
                    dve.wait_ge(exp_ready, half + 1)
                    link(nc.vector.scalar_tensor_tensor(out=mix, in0=marked, scalar=SENT, in1=e, op0=ALU.is_equal, op1=ALU.mult))
                    link(nc.vector.reduce_sum(total, mix, AX_X))
                    link(nc.vector.reciprocal(inverse, total))
                    nc.vector.tensor_tensor(mix, mix, inverse.unsqueeze(2).broadcast_to([P, mix.shape[1], NE]), ALU.mult).then_inc(mix_ready, 1)

                def expert_weights_low(hi, lo, n):
                    dve.wait_ge(w_hi_ready, n)
                    nc.vector.tensor_tensor(lo[:], w_raw[:], hi[:], ALU.subtract).then_inc(w_lo_ready, 1)

                def chunk(it, k, between=None):
                    n = k + 1
                    at_chunk[:] = [it, k, 0]
                    normalize(it, k, 0)
                    normalize(it, k, 1)
                    key_diagonal(it, k)
                    normalize(it, k, 2)
                    normalize(it, k, 3)
                    if between:
                        between()
                    mask_scores(it, n, 0)
                    mask_scores(it, n, 1)
                    add_residual(it, k)
                    norm(it, k)
                    mask_scores(it, n, 2)
                    mask_scores(it, n, 3)
                    take_keys(it, n)
                    take_routes(it, k)
                    choose(it, k)
                    assert at_chunk[2] == PER

                for g in range(NG):
                    mask_scores(0, 0, g)
                take_keys(0, 0)
                dve.wait_ge(in_routers, 16 * 3)
                nc.vector.tensor_copy(zc[:, :, NE:ZW], sent_sb[:]).then_inc(init_v, 1)
                dve.wait_ge(rw_done, 1)
                dve.wait_ge(init_v, N_INIT_V)
                nc.vector.tensor_copy(route_w[:, 0:NR * NE], out_bank[0][:, 0:NR * NE]).then_inc(rw_ready, 1)
                with dve.Fori(0, NIT - 1) as it:
                    for k in range(BODY):
                        chunk(it, k)
                for k in range(BODY - 1):
                    chunk(NIT - 1, k, between=(lambda: (routing_shift(0), expert_weights_low(w1_hi, w1_lo, 1)),
                                               lambda: routing_weights(0),
                                               lambda: expert_weights_low(w2_hi, w2_lo, 2))[k])

                dve.sem_inc(mixed1, DVE_E)
                dve.sem_inc(mixed2, DVE_E)
                dve.sem_inc(ysum_ready, 1)

                def mixture(it, k, r, banks, done_sem, acc, mixed, experts, seeds=(None, None)):
                    if experts[0] == 0:
                        dve.wait_ge(cw_ready, count(it, k, 1, 1))
                    for e in experts:
                        if e % EU == 0:
                            dve.wait_ge(done_sem, count(it, k, NU, e // EU + 2))
                        src = banks[e // EU][:, (e % EU) * D:(e % EU + 1) * D]
                        a, w = acc[:, e % 2, :], cw[k % BODY][:, r * NE + e:r * NE + e + 1]
                        if e >= 2:
                            dve.wait_ge(mixed, count(it, k, DVE_E, DVE_E + e - 1))
                            ins = nc.vector.scalar_tensor_tensor(out=a, in0=src, scalar=w, in1=a, op0=ALU.mult, op1=ALU.add)
                        elif seeds[e] is not None:
                            ins = nc.vector.scalar_tensor_tensor(out=a, in0=src, scalar=w, in1=seeds[e], op0=ALU.mult, op1=ALU.add)
                        else:
                            ins = nc.vector.tensor_scalar(a, src, w, None, ALU.mult)
                        ins.then_inc(mixed, 1)

                def hidden(it, k, experts, first=False):
                    if experts[0] == 0 and (not first or k):
                        dve.wait_ge(hsum_ready, count(it, k, 1, 0))
                    mixture(it, k, 0, bank[0:2], l1_done, acc1, mixed1, experts)

                def output_mixture(it, k):
                    dve.wait_ge(b2_ready, count(it, k, 1, 1))
                    mixture(it, k, 1, bank[3:5], l2_done, acc2, mixed2, range(DVE_E), seeds=(row(x1_all, it, k), c3b2[:]))
                    dve.wait_ge(mixed2, count(it, k, DVE_E, 2 * DVE_E))
                    nc.vector.tensor_tensor(pair2[:], acc2[:, 0, :], acc2[:, 1, :], ALU.add).then_inc(pair2_ready, 1)

                def output_total(it, k):
                    dve.wait_ge(pair2_ready, count(it, k, 1, 1))
                    dve.wait_ge(rest2_ready, count(it, k, 1, 2))
                    dve.sem_inc(passed, 1)
                    nc.vector.tensor_tensor(row(x1_all, it, k), pair2[:], rest2[:], ALU.add).then_inc(ysum_ready, 1)

                def output_stats(it, k):
                    dve.wait_ge(ysum_ready, count(it, k, 1, 2))
                    dve.sem_inc(passed, 1)
                    nc.vector.bn_stats(ostats[:], row(x1_all, it, k)).then_inc(ostep, 1)

                def output_variance(it, k):
                    dve.wait_ge(ostep, count(it, k, 2, 1))
                    dve.sem_inc(passed, 1)
                    nc.vector.bn_aggr(omv_c[:], ostats[:]).then_inc(ostep, 1)

                def keep_variance(it, k):
                    dve.wait_ge(ostep, count(it, k, 2, 2))
                    nc.vector.tensor_copy(row(omv, it, k), omv_c[:]).then_inc(ovar_ready, 1)

                def outputs(half):
                    c = SPLIT[half]
                    dve.wait_ge(osd_ready, half + 1)
                    nc.vector.reciprocal(ors[:, c], osd[:, c]).then_inc(ors_ready, 1)
                    dve.wait_ge(ors_ready, half + 1)
                    for i in range(c.start, c.stop):
                        nc.vector.tensor_scalar(x1_all[:, i], x1_all[:, i], omv[:, i, 0:1], ors[:, i:i + 1], ALU.subtract, ALU.mult)\
                          .then_inc(oc_ready, 1)

                def expert_chunk(it, k, left):
                    output_mixture(it, k)
                    for i, finish in enumerate((output_total, output_stats, output_variance, keep_variance)):
                        if left >= 2:
                            hidden(it, k + 2, range(2 * i, 2 * i + 2))
                        finish(it, k)

                last = (NIT - 1, BODY - 1)
                at_chunk[:] = [*last, 0]
                for g in range(NG):
                    normalize(*last, g)
                add_residual(*last)
                norm(*last)
                hidden(0, 0, range(DVE_E), first=True)
                take_routes(*last)
                hidden(0, 1, range(DVE_E), first=True)
                choose(*last)
                routing_shift(1)
                dve.wait_ge(x1_saved, NCH + 1)
                routing_weights(1)
                with dve.Fori(0, NIT - 1) as it:
                    for k in range(BODY):
                        expert_chunk(it, k, BODY)
                for k in range(BODY):
                    expert_chunk(NIT - 1, k, BODY - 1 - k)
                    if k == BODY - 2:
                        outputs(0)
                outputs(1)

            @block.gpsimd
            def _(pool):
                nc.gpsimd.memset(zeros[:], 0.0)
                nc.gpsimd.memset(st[:], 0.0).then_inc(init_g, 1)
                nc.gpsimd.memset(sx[:], 0.0).then_inc(init_g, 1)
                nc.gpsimd.memset(v1[:], 0.0).then_inc(init_g, 1)
                nc.gpsimd.memset(kf[:], 0.0).then_inc(init_g, 1)
                nc.gpsimd.memset(b2_sb[:], 0.0).then_inc(init_g, 1)
                for b in range(BODY):
                    ms = nc.gpsimd.memset(cw[b][:], 0.0)
                ms.then_inc(init_g, 1)
                pool.wait_ge(init_g, N_INIT_G - 1)
                nc.gpsimd.memset(v1[:, :, DV], 1.0).then_inc(init_g, 1)
                pool.sem_inc(kp_ready, 1)
                pool.sem_inc(x1_saved, 1)
                pool.sem_inc(x1t_saved, 1)
                pool.wait_ge(init_g, N_INIT_G)
                pool.dma_start(b2_sb[2 * NE:3 * NE, :], b2).then_inc(in_b2, 16)

                pool.sem_inc(low_ready_g, 3)
                with pool.Fori(0, T // GRP // 2) as gg:
                    for b in range(2):
                        for t in (1, 2, 3):
                            pool.wait_ge(mid_ready_v if t == 2 else mid_ready_a, gg * 4 + (2 * b + t // 2 + 1))
                            nc.gpsimd.tensor_tensor(low[b][:, t, :], rem[:, t, :], mid[b][:, t, :], ALU.subtract).then_inc(low_ready_g, 1)

                def take_x(it, k, first=False):
                    if not first:
                        pool.wait_ge(kv_done, count(it, k, 3, 0))
                    nc.gpsimd.tensor_copy(x_hi[:], columns(xT_all, it, k)).then_inc(x_parts_ready, 1)
                    pool.wait_ge(x_parts_ready, count(it, k, 2, 1))
                    pool.sem_inc(passed_g, 1)
                    nc.gpsimd.tensor_tensor(x_lo[:], columns(xT_all, it, k), x_hi[:], ALU.subtract).then_inc(x_parts_ready, 1)

                def key_products(it, k):
                    pool.wait_ge(k2_ready, count(it, k, 1, 2))
                    whole = k2[:]
                    ahead = bass.AP(whole.tensor, whole.offset + 1,
                                    [whole.ap[0], (2 * NA, NH), (1, NF // NA - 1), (1, NA)])
                    here = k2[:, :, 0:NA].unsqueeze(2).broadcast_to([P, NH, NF // NA - 1, NA])
                    out4 = kf[:, :, NA:NF].rearrange("p h (d i) -> p h d i", i=NA)
                    nc.gpsimd.tensor_tensor(out4, here, ahead, ALU.mult).then_inc(kp_ready, 1)

                def keep_x1(it, k):
                    pool.wait_ge(x1_ready, count(it, k, 1, 1))
                    nc.gpsimd.tensor_copy(row(x1_all, it, k), x1c[:]).then_inc(x1_saved, 1)
                    pool.wait_ge(x1t_ready, count(it, k, 1, 2))
                    nc.gpsimd.tensor_copy(columns(x1T_all, it, k), x1T[:]).then_inc(x1t_saved, 1)

                pool.wait_ge(in_qk, 32)
                pool.wait_ge(in_xT, 16)
                take_x(0, 0, first=True)
                pool.wait_ge(init_v, 3)
                key_products(0, 0)
                with pool.Fori(0, NIT - 1) as it:
                    for k in range(BODY):
                        take_x(it, k + 1)
                        keep_x1(it, k)
                        key_products(it, k + 1)
                for k in range(BODY - 1):
                    take_x(NIT - 1, k + 1)
                    keep_x1(NIT - 1, k)
                    key_products(NIT - 1, k + 1)

                pool.sem_inc(half1_ready, 1)
                pool.sem_inc(rest2_ready, 1)
                at_chunk = [0, 0, 0]

                def step(ins):
                    it, k, n = at_chunk
                    ins.then_inc(sum_step, 1)
                    at_chunk[2] = n + 1
                    pool.wait_ge(sum_step, BEFORE + count(it, k, PER, n + 1) if it is not None else n + 1)

                PER, BEFORE = 3, 4

                def hidden_low(it, k, first=False):
                    pool.wait_ge(took, count(it, k, 3, 5))
                    if not first:
                        pool.wait_ge(l2_done, count(it, k, NU, 0))
                    nc.gpsimd.tensor_tensor(hT_lo[:], hT[:], hT_hi[:], ALU.subtract).then_inc(h_lo_ready, 1)

                def x1_low(it, k):
                    pool.wait_ge(x1_hi_ready, count(it, k, 1, 1))
                    nc.gpsimd.tensor_tensor(xb_lo[k % 2][:], xb[k % BODY][:], xb_hi[k % 2][:], ALU.subtract).then_inc(x1_lo_ready, 1)

                def stage_weights(it, k, first=False):
                    if first:
                        pool.wait_ge(mix_ready, 1)
                    else:
                        pool.wait_ge(mixed2, count(it, k, DVE_E, -2 * DVE_E))
                        pool.wait_ge(prod2_ready, count(it, k, 1, -2))
                    nc.gpsimd.tensor_copy(cw[k % BODY][:, 0:NR * NE], row(mix_all, it, k).rearrange("p r e -> p (r e)"))\
                      .then_inc(cw_ready, 1)

                def hidden_rest(it, k):
                    pool.wait_ge(prod1_ready, count(it, k, 1, 2))
                    step(nc.gpsimd.tensor_tensor(half1[:], prod1[:, 0:2, :], prod1[:, 2:4, :], ALU.add))
                    nc.gpsimd.tensor_tensor(rest1[:], half1[:, 0, :], half1[:, 1, :], ALU.add).then_inc(half1_ready, 1)

                def hidden_sum(it, k, first=False):
                    pool.wait_ge(mixed1, count(it, k, DVE_E, 2 * DVE_E))
                    step(nc.gpsimd.tensor_tensor(pair1[:], acc1[:, 0, :], acc1[:, 1, :], ALU.add))
                    pool.wait_ge(half1_ready, count(it, k, 1, 2))
                    if not first:
                        pool.wait_ge(h_ready, count(it, k, 1, -1))
                    nc.gpsimd.tensor_tensor(hsum[k % 2][:], pair1[:], rest1[:], ALU.add).then_inc(hsum_ready, 1)

                def output_rest(it, k):
                    pool.wait_ge(prod2_ready, count(it, k, 1, 2))
                    step(nc.gpsimd.tensor_tensor(half2[:], prod2[:, 0:2, :], prod2[:, 2:4, :], ALU.add))
                    pool.wait_ge(ysum_ready, count(it, k, 1, 1))
                    nc.gpsimd.tensor_tensor(rest2[:], half2[:, 0, :], half2[:, 1, :], ALU.add).then_inc(rest2_ready, 1)

                pool.wait_ge(in_w1, 16)
                pool.wait_ge(s_done, NG * NCH)
                for k in range(BODY):
                    stage_weights(0, k, first=True)
                x1_low(0, 0)
                x1_low(0, 1)
                at_chunk[:] = [None, 0, 0]
                hidden_rest(0, 0)
                hidden_sum(0, 0, first=True)
                keep_x1(NIT - 1, BODY - 1)
                hidden_low(0, 0, first=True)
                hidden_rest(0, 1)
                x1_low(0, 2)
                hidden_sum(0, 1, first=True)
                pool.wait_ge(mix_ready, 2)
                with pool.Fori(0, NIT - 1) as it:
                    for k in range(BODY):
                        at_chunk[:] = [it, k, 0]
                        output_rest(it, k)
                        hidden_low(it, k + 1)
                        hidden_rest(it, k + 2)
                        x1_low(it, k + 3)
                        hidden_sum(it, k + 2)
                        stage_weights(it, k + BODY)
                        assert at_chunk[2] == PER
                for k in range(BODY):
                    at_chunk[:] = [NIT - 1, k, 0 if k < BODY - 1 else -2]
                    output_rest(NIT - 1, k)
                    if k + 1 < BODY:
                        hidden_low(NIT - 1, k + 1)
                    if k + 2 < BODY:
                        hidden_rest(NIT - 1, k + 2)
                    if k + 3 < BODY:
                        x1_low(NIT - 1, k + 3)
                    if k + 2 < BODY:
                        hidden_sum(NIT - 1, k + 2)


def kernel(**inputs):
    import concourse.bacc as bacc
    from concourse.bass_utils import run_bass_kernel_spmd

    a = {n.removeprefix("L0_"): np.asarray(v) for n, v in inputs.items()}
    x = np.ascontiguousarray(a["attn_hidden_states"].reshape(T, D))
    consts, sents = shape_constants()
    arrays = {
        "x": x,
        "xT": np.ascontiguousarray(x.T),
        "wqk": np.concatenate([a["attn_Wq"], a["attn_Wk"]], axis=1),
        "wkv": np.concatenate([a["attn_Wv"], a["attn_Wk"]], axis=1),
        "wo": np.ascontiguousarray(a["attn_Wo"]),
        "p_w": np.ascontiguousarray(a["ffn_P_w"]),
        "uT": np.ascontiguousarray(np.concatenate([a["ffn_U1"], a["ffn_U2"], a["ffn_U3"]], axis=0).T),
        "w1T": np.ascontiguousarray(a["ffn_W1"].transpose(2, 0, 1).reshape(D, NE * D)),
        "w2T": np.ascontiguousarray(a["ffn_W2"].transpose(2, 0, 1).reshape(D, NE * D)),
        "b2": np.ascontiguousarray(a["ffn_b2"]),
        "consts": consts,
        "sents": sents,
    }
    nc = bacc.Bacc("TRN2", target_bir_lowering=False, num_devices=1)
    handles = [nc.dram_tensor(n, list(v.shape), F32, kind="ExternalInput").ap() for n, v in arrays.items()]
    out = nc.dram_tensor("out", [T, D], F32, kind="ExternalOutput").ap()
    block_kernel(nc, *handles, out)
    r = run_bass_kernel_spmd(nc, [arrays], core_ids=[0])
    return r.results[0]["out"].reshape(1, T, D)
```
